# Optimizing a Trainium2 kernel written in Bass

```python
import numpy as np
import jax
import jax.numpy as jnp

def _softmax(x, axis=-1):
    return jax.nn.softmax(x, axis=axis)

def _gelu(x):
    return jax.nn.gelu(x, approximate=True)

def _silu(x):
    return jax.nn.silu(x)

def _sigmoid(x):
    return jax.nn.sigmoid(x)

def _layernorm(x, axis=-1, eps=1e-05):
    m = jnp.mean(x, axis=axis, keepdims=True)
    v = jnp.var(x, axis=axis, keepdims=True)
    return (x - m) / jnp.sqrt(v + eps)

def _scatter_add(tgt, idx, src, axis=0):
    return tgt.at[idx].add(src)

def _segment_sum(src, seg, n):
    return jax.ops.segment_sum(src, seg, n)
kernel_name = 'mk_xattn_seq_d2_seqx_r8_a4de69'

def setup_inputs(seed: int=0):
    np.random.seed(seed)
    _w = jnp.asarray

    def _rec_inputs():
        import jax
        import jax.numpy as jnp
        _rk = jax.random.key(seed)
        x = -0.000125 + 0.9999 * jax.random.normal(jax.random.fold_in(_rk, 1), (4, 256, 256), jnp.float32)
        _lenS = 256 - jax.random.randint(jax.random.fold_in(_rk, 7), (4,), 0, max(1, 256 // 4) + 1, jnp.int32)
        _lenS2 = 512 - jax.random.randint(jax.random.fold_in(_rk, 8), (4,), 0, max(1, 512 // 4) + 1, jnp.int32)
        _ctx_1024P = jax.random.normal(jax.random.fold_in(_rk, 11), (4, 16, 128), jnp.float32)
        _ctx_1024c = jax.random.dirichlet(jax.random.fold_in(_rk, 511), 0.3 * jnp.ones((16,), jnp.float32), (4, 512))
        _ctx_1024t = jnp.einsum('bsk,bkd->bsd', _ctx_1024c, _ctx_1024P)
        _ctx_1024t = _ctx_1024t * jax.lax.rsqrt(jnp.mean(jnp.square(_ctx_1024t)) + 1e-12) * 0.953939
        ctx_1024 = 4.13588e-05 + 0.999923 * (_ctx_1024t + 0.3 * jax.random.normal(jax.random.fold_in(_rk, 611), (4, 512, 128), jnp.float32))
        _validS = jnp.arange(256)[None, :] < _lenS[:, None]
        _validS2 = jnp.arange(512)[None, :] < _lenS2[:, None]
        _causal = jnp.tril(jnp.ones((256, 256), dtype=bool))
        mask_BxS2_bk0 = jnp.logical_not(jnp.broadcast_to(_validS2[:, :], (4, 512)))
        return (x, ctx_1024, mask_BxS2_bk0)
    x, ctx_1024, mask_BxS2_bk0 = _rec_inputs()

    def _L0_xattn_setup():
        import jax, jax.numpy as jnp
        import numpy as np
        EPS = 1e-06

        def _rmsnorm(x, w):
            var = jnp.mean(jnp.square(x), axis=-1, keepdims=True)
            return x * jax.lax.rsqrt(var + EPS) * w
        key = jax.random.key(seed)
        ks = jax.random.split(key, 6)
        B, N, M = (4, 512, 256)
        d_model, memory_dim = (256, 128)
        hidden_states = jax.random.normal(ks[0], (B, N, d_model), dtype=jnp.float32)
        memory = jax.random.normal(ks[1], (B, M, memory_dim), dtype=jnp.float32)
        W_mem = jax.random.normal(ks[2], (d_model, memory_dim), dtype=jnp.float32) / np.sqrt(memory_dim)
        W_gate = jax.random.normal(ks[3], (d_model, 2 * d_model), dtype=jnp.float32) / np.sqrt(2 * d_model)
        b_gate = jax.random.normal(ks[4], (d_model,), dtype=jnp.float32) * 0.01
        norm_w = jnp.ones((d_model,), dtype=jnp.float32)
        return {'hidden_states': hidden_states, 'memory': memory, 'W_mem': W_mem, 'W_gate': W_gate, 'b_gate': b_gate, 'norm_w': norm_w}
    _L0_xattn_all = _L0_xattn_setup()
    _L0_xattn_in = {k: v for k, v in _L0_xattn_all.items() if k in ('W_mem', 'W_gate', 'b_gate', 'norm_w')}
    del _L0_xattn_all

    def _L1_xattn_setup():
        import jax, jax.numpy as jnp
        import numpy as np
        DIM = 256
        DIM_MEDIA = 128
        HEADS = 16
        DIM_HEAD = 64
        INNER = HEADS * DIM_HEAD
        FF_INNER = 4 * DIM
        B, N_TOK, N_LAT = (4, 256, 64)
        EPS = 1e-05

        def layernorm(x, g, b):
            mu = jnp.mean(x, axis=-1, keepdims=True)
            var = jnp.var(x, axis=-1, keepdims=True)
            return (x - mu) * jax.lax.rsqrt(var + EPS) * g + b
        key = jax.random.key(seed)
        ks = jax.random.split(key, 12)
        x = jax.random.normal(ks[0], (B, N_TOK, DIM), dtype=jnp.float32)
        media = jax.random.normal(ks[1], (B, N_LAT, DIM_MEDIA), dtype=jnp.float32)
        media_mask = jax.random.randint(ks[2], (B, N_LAT), 0, 2).astype(bool)
        media_mask = media_mask.at[:, 0].set(True)
        s = lambda d: 1.0 / np.sqrt(d)
        Wq = jax.random.normal(ks[3], (DIM, INNER), dtype=jnp.float32) * s(DIM)
        Wkv = jax.random.normal(ks[4], (DIM_MEDIA, 2 * INNER), dtype=jnp.float32) * s(DIM_MEDIA)
        Wo = jax.random.normal(ks[5], (INNER, DIM), dtype=jnp.float32) * s(INNER)
        W1 = jax.random.normal(ks[6], (DIM, FF_INNER), dtype=jnp.float32) * s(DIM)
        W2 = jax.random.normal(ks[7], (FF_INNER, DIM), dtype=jnp.float32) * s(FF_INNER)
        return {'x': x, 'media': media, 'media_mask': media_mask, 'ln_q_g': jnp.ones((DIM,), jnp.float32), 'ln_q_b': jnp.zeros((DIM,), jnp.float32), 'Wq': Wq, 'Wkv': Wkv, 'Wo': Wo, 'attn_gate': jax.random.normal(ks[8], (1,), jnp.float32) * 0.5, 'ln_ff_g': jnp.ones((DIM,), jnp.float32), 'ln_ff_b': jnp.zeros((DIM,), jnp.float32), 'W1': W1, 'W2': W2, 'ff_gate': jax.random.normal(ks[9], (1,), jnp.float32) * 0.5}
    _L1_xattn_all = _L1_xattn_setup()
    _L1_xattn_in = {k: v for k, v in _L1_xattn_all.items() if k in ('ln_q_g', 'ln_q_b', 'Wq', 'Wkv', 'Wo', 'attn_gate', 'ln_ff_g', 'ln_ff_b', 'W1', 'W2', 'ff_gate')}
    del _L1_xattn_all
    return {'x': x, 'ctx_1024': ctx_1024, 'mask_BxS2_bk0': mask_BxS2_bk0, 'L0_xattn_W_mem': _L0_xattn_in['W_mem'], 'L0_xattn_W_gate': _L0_xattn_in['W_gate'], 'L0_xattn_b_gate': _L0_xattn_in['b_gate'], 'L0_xattn_norm_w': _L0_xattn_in['norm_w'], 'L1_xattn_ln_q_g': _L1_xattn_in['ln_q_g'], 'L1_xattn_ln_q_b': _L1_xattn_in['ln_q_b'], 'L1_xattn_Wq': _L1_xattn_in['Wq'], 'L1_xattn_Wkv': _L1_xattn_in['Wkv'], 'L1_xattn_Wo': _L1_xattn_in['Wo'], 'L1_xattn_attn_gate': _L1_xattn_in['attn_gate'], 'L1_xattn_ln_ff_g': _L1_xattn_in['ln_ff_g'], 'L1_xattn_ln_ff_b': _L1_xattn_in['ln_ff_b'], 'L1_xattn_W1': _L1_xattn_in['W1'], 'L1_xattn_W2': _L1_xattn_in['W2'], 'L1_xattn_ff_gate': _L1_xattn_in['ff_gate']}

def reference(x, ctx_1024, mask_BxS2_bk0, L0_xattn_W_mem, L0_xattn_W_gate, L0_xattn_b_gate, L0_xattn_norm_w, L1_xattn_ln_q_g, L1_xattn_ln_q_b, L1_xattn_Wq, L1_xattn_Wkv, L1_xattn_Wo, L1_xattn_attn_gate, L1_xattn_ln_ff_g, L1_xattn_ln_ff_b, L1_xattn_W1, L1_xattn_W2, L1_xattn_ff_gate):
    import jax
    import jax.numpy as jnp

    def _L0_xattn_ref(hidden_states, memory, W_mem, W_gate, b_gate, norm_w):
        import jax, jax.numpy as jnp
        import numpy as np
        EPS = 1e-06

        def _rmsnorm(x, w):
            var = jnp.mean(jnp.square(x), axis=-1, keepdims=True)
            return x * jax.lax.rsqrt(var + EPS) * w
        D = hidden_states.shape[-1]
        memory_proj = jnp.einsum('bme,de->bmd', memory, W_mem)
        scores = jnp.einsum('bnd,bmd->bnm', hidden_states, memory_proj) / jnp.sqrt(jnp.float32(D))
        attn = jax.nn.softmax(scores, axis=-1)
        memory_context = jnp.einsum('bnm,bmd->bnd', attn, memory_proj)
        gate_input = jnp.concatenate([hidden_states, memory_context], axis=-1)
        gate = jax.nn.sigmoid(jnp.einsum('bnf,df->bnd', gate_input, W_gate) + b_gate)
        fused = hidden_states + gate * memory_context
        return _rmsnorm(fused, norm_w)

    def _L1_xattn_ref(x, media, media_mask, ln_q_g, ln_q_b, Wq, Wkv, Wo, attn_gate, ln_ff_g, ln_ff_b, W1, W2, ff_gate):
        import jax, jax.numpy as jnp
        import numpy as np
        DIM = 256
        DIM_MEDIA = 128
        HEADS = 16
        DIM_HEAD = 64
        INNER = HEADS * DIM_HEAD
        FF_INNER = 4 * DIM
        B, N_TOK, N_LAT = (4, 256, 64)
        EPS = 1e-05

        def layernorm(x, g, b):
            mu = jnp.mean(x, axis=-1, keepdims=True)
            var = jnp.var(x, axis=-1, keepdims=True)
            return (x - mu) * jax.lax.rsqrt(var + EPS) * g + b
        scale = DIM_HEAD ** (-0.5)
        qn = layernorm(x, ln_q_g, ln_q_b)
        q = qn @ Wq * scale
        kv = media @ Wkv
        k, v = jnp.split(kv, 2, axis=-1)
        split_heads = lambda t: t.reshape(t.shape[0], t.shape[1], HEADS, DIM_HEAD).transpose(0, 2, 1, 3)
        q, k, v = (split_heads(q), split_heads(k), split_heads(v))
        sim = jnp.einsum('bhid,bhjd->bhij', q, k)
        neg_inf = jnp.finfo(sim.dtype).min
        sim = jnp.where(media_mask[:, None, None, :], sim, neg_inf)
        attn = jax.nn.softmax(sim, axis=-1)
        out = jnp.einsum('bhij,bhjd->bhid', attn, v)
        out = out.transpose(0, 2, 1, 3).reshape(x.shape[0], x.shape[1], INNER)
        attn_out = out @ Wo
        x = x + jnp.tanh(attn_gate) * attn_out
        h = layernorm(x, ln_ff_g, ln_ff_b)
        h = jax.nn.gelu(h @ W1, approximate=False) @ W2
        x = x + jnp.tanh(ff_gate) * h
        return x
    x = _L0_xattn_ref(x, ctx_1024, L0_xattn_W_mem, L0_xattn_W_gate, L0_xattn_b_gate, L0_xattn_norm_w)
    x = _L1_xattn_ref(x, ctx_1024, mask_BxS2_bk0, L1_xattn_ln_q_g, L1_xattn_ln_q_b, L1_xattn_Wq, L1_xattn_Wkv, L1_xattn_Wo, L1_xattn_attn_gate, L1_xattn_ln_ff_g, L1_xattn_ln_ff_b, L1_xattn_W1, L1_xattn_W2, L1_xattn_ff_gate)
    return x

_drawn_inputs = setup_inputs


def setup_inputs(seed=0):
    import zlib

    import numpy as np

    out = dict(_drawn_inputs(seed))
    spreads = {'L0_xattn_norm_w': (1.0, 0.2),
     'L1_xattn_ln_q_g': (1.0, 0.6),
     'L1_xattn_ln_q_b': (0.0, 0.8),
     'L1_xattn_ln_ff_g': (1.0, 0.6),
     'L1_xattn_ln_ff_b': (0.0, 0.8)}
    factors = {'L0_xattn_b_gate': 52.309, 'L1_xattn_W1': 2.744}
    for name, (base, spread) in spreads.items():
        noise = np.random.default_rng([zlib.crc32(name.encode()), seed]).standard_normal(out[name].shape)
        drawn = base * np.exp(spread * noise) if base else spread * noise
        out[name] = jnp.asarray(drawn.astype(out[name].dtype))
    for name, factor in factors.items():
        out[name] = (out[name] * factor).astype(out[name].dtype)
    return out
```

```python
from contextlib import ExitStack

import concourse.bass as bass
from concourse import mybir

F32 = mybir.dt.float32
F32R = mybir.dt.float32r
BF16 = mybir.dt.bfloat16
U8 = mybir.dt.uint8
I32 = mybir.dt.int32
ALU = mybir.AluOpType
ACT = mybir.ActivationFunctionType
AX_X = mybir.AxisListType.X

P = 128
BANK = 512
HI, LO = 0, 1
MASKED = -(2.0 ** 100)
RMS_EPS = 1e-6
LN_EPS = 1e-5


def gated_attention_block(nc, x, ctx_in, mask, w_mem, w_gate, b_gate, norm_w, lnq_g, lnq_b, wq, wkv, wo,
                          attn_gate, lnf_g, lnf_b, w1, w2, ff_gate, out):
    B, N, D = x.shape
    M, E = ctx_in.shape[1:]
    INNER = wq.shape[1]
    FF = w1.shape[1]
    DH = 64
    H = INNER // DH
    T = N // P
    KT = M // P
    K = D // P
    PAIRS = H // 2
    FM = FF // P
    HOT = KT - 1
    assert (T, KT, K, DH * 2, D, E) == (2, 4, 2, P, 2 * P, P)

    def prologue():
        yield ("xT", 0)
        yield ("ctxT", 0)
        yield ("weights",)
        yield ("y", 0)
        yield ("scores", "ctx", 0, 0)
        yield ("ctxT", 1)
        yield ("ctxT", 2)
        yield ("ctxT", 3)
        yield ("qbias",)
        yield ("splitq",)
        yield ("norm", "ctx", 0, 0)
        yield ("spread", "ctx", 0, 0)
        yield ("u", 0)
        yield ("gate", 0)
        yield ("fuse", 0)
        yield ("rms", 0)
        yield ("ln1", 0)
        yield ("splito",)
        yield ("xhat", 0)
        yield ("xhT", 0)

    def body(nt):
        units = 4 * nt
        lines = []
        for b in range(B):
            for u in range(units):
                lines.append(("head", b, u))
                if u == 1 and b + 1 < B:
                    lines.append(("ctx", b + 1, 0))
        held = None
        quads_q = units // 4
        for b in range(B):
            if nt > 1 or b == 0:
                for pair in range(PAIRS):
                    yield ("k", b, pair)
                for s in range(KT):
                    yield ("v", b, s, 0)
                    yield ("v", b, s, 1)
            if b == 0:
                yield ("q", b, 0)
            for u in range(units):
                yield ("scores", "head", b, u)
                if u == 0 and b + 1 < B:
                    yield ("xT", b + 1)
                if held:
                    yield from second(held, nt)
                held = ("head", b, u)
                if u % quads_q == quads_q - 1 and u // quads_q + 1 < 4:
                    yield ("q", b, u // quads_q + 1)
                if u == 0:
                    if b + 1 < B:
                        yield ("y", b + 1)
                    if b:
                        yield ("wo", b - 1)
                if u == 1:
                    if b:
                        yield ("ln2", b - 1)
                    if b + 1 < B:
                        yield ("scores", "ctx", b + 1, 0)
                        yield from second(held, nt)
                        held = ("ctx", b + 1, 0)
                if u == 2 and b + 1 < B:
                    yield ("gate", b + 1)
                    yield ("fuse", b + 1)
                if u == 3 and b + 1 < B:
                    yield ("rms", b + 1)
                    yield ("ln1", b + 1)
                if nt > 1 and u == units - 1:
                    yield from second(held, nt)
                    held = None
            if b + 1 < B:
                yield ("xhat", b + 1)
                yield ("xhT", b + 1)
                yield ("q", b + 1, 0)
            if b == 0:
                yield ("w1load",)
        if held:
            yield from second(held, nt)
        yield ("split1",)
        yield ("wo", B - 1)
        yield ("ln2", B - 1)
        for f in range(B // 2):
            for half in range(2):
                yield ("x2hat", 2 * f + half)
                yield ("h2T", f, half)
            if f == 0:
                yield ("split2",)
            for m in range(FM):
                yield ("ff1", f, m)
            for i in range(2 * T):
                yield ("ff2", f, i)

    def second(item, nt):
        kind, b, u = item
        yield ("norm", kind, b, u)
        yield ("spread", kind, b, u)
        if kind == "ctx":
            yield ("u", b)
        else:
            yield ("av", b, u)

    with ExitStack() as stack:
        def sb(name, shape, dt=F32):
            return stack.enter_context(nc.sbuf_tensor(name, shape, dt))

        def sem(name):
            return stack.enter_context(nc.semaphore(name))

        def psum(name, shape):
            return stack.enter_context(nc.psum_tensor(name, shape, F32))

        ident = sb("ident", [P, P])
        ones_row = sb("ones_row", [1, P])
        ones_bf = sb("ones_bf", [1, P], BF16)
        mask_u8 = sb("mask_u8", [1, B * M], U8)
        mask_bias = sb("mask_bias", [1, B * M], BF16)
        tile_any = sb("tile_any", [1, B * KT])
        flag_work = sb("flag_work", [1, 4 * B])
        short_flag = sb("short_flag", [1, 1], I32)
        x_sb = sb("x_sb", [P, B * T, D])
        ctx_sb = sb("ctx_sb", [P, B * KT, E])
        ctxT = sb("ctxT", [P, B, M])
        wmem_sb = sb("wmem_sb", [P, K, E])
        wgate_sb = sb("wgate_sb", [P, K, 2 * D])
        gate_xT = sb("gate_xT", [P, K, D])
        gate_cT = sb("gate_cT", [P, K, D])
        gate_mem = sb("gate_mem", [P, 2 * D])
        bgate_row = sb("bgate_row", [1, D])
        normw_sb = sb("normw_sb", [P, D])
        lncol = sb("lncol", [P, 4, K])
        gates = sb("gates", [P, 4])
        q_scale = sb("q_scale", [P, K])
        q_bias = sb("q_bias", [P, PAIRS])
        h_bias = sb("h_bias", [P, FM])
        half_pow = sb("half_pow", [P, T])
        stage = sb("stage", [P, 2048])
        wkv_sb = sb("wkv_sb", [P, 2 * INNER])
        wq_pair = sb("wq_pair", [P, 2, 2048], F32R)
        wo_pair = sb("wo_pair", [P, 2, 2048], F32R)
        th = sb("th", [P, T, D])
        fused = sb("fused", [P, T, D])
        xhat = sb("xhat", [P, T, D])
        xhT_pair = sb("xhT_pair", [P, 2, K, N], F32R)
        stats = sb("stats", [P, T, 6])
        mean_var = sb("mean_var", [P, T, 2])
        mean_var2 = sb("mean_var2", [P, B * T, 2])
        sumsq = sb("sumsq", [P, T])
        ms = sb("ms", [P, T])
        rms_r = sb("rms_r", [P, T])
        ve = sb("ve", [P, T])
        rstd = sb("rstd", [P, T])
        ve2 = sb("ve2", [P, B, T])
        rstd2 = sb("rstd2", [P, B, T])
        q_sb = sb("q_sb", [P, PAIRS, N])
        RING = 4
        neg_max = sb("neg_max", [P, RING, 4])
        row_sum = sb("row_sum", [P, RING, 4])
        row_rcp = sb("row_rcp", [P, RING, 4])
        expd = sb("expd", [P, RING, BANK])
        probs = sb("probs", [P, RING, BANK])
        probsT = sb("probsT", [P, 2, 4, N])
        oT_pair = sb("oT_pair", [P, 2, PAIRS, N], F32R)

        l0_start = nc.sbuf_base
        l0_region = sb("l0_region", [P, 2048])
        xT = l0_region[:, 0:512].rearrange("p (k n) -> p k n", k=K)
        ctx_probsT = l0_region[:, 512:1536].rearrange("p (k n) -> p k n", k=KT)
        yT = l0_region[:, 1536:1792]
        uT = l0_region[:, 1792:2048]
        kv_start = nc.sbuf_base
        k_split = sb("k_split", [P, PAIRS, KT, 2, P])
        v_sb = sb("v_sb", [P, KT, INNER])
        w2_pair = nc.alloc_sbuf_tensor_at("w2_pair", [P, 2, FM, D], F32R, offset=kv_start)
        gelu_pair = nc.alloc_sbuf_tensor_at("gelu_pair", [P, 2, FM, 2 * N], F32R, offset=kv_start + 16384)
        h2T_pair = nc.alloc_sbuf_tensor_at("h2T_pair", [P, 2, K, 2 * N], F32R, offset=l0_start)

        bank = [psum(f"bank{i}", [P, BANK]) for i in range(8)]
        GEN, SC, SPREAD, CONTEXT = bank[0:3], bank[3:5], bank[5:7], bank[7]

        wq_raw = stage[:, :].rearrange("p (k n) -> p k n", k=K)
        wq_p = wq_pair[:, :, :].rearrange("p h (k n) -> p h k n", k=K)
        w1_p = wq_p
        wo_p = wo_pair[:, :, :].rearrange("p h (i n) -> p h i n", n=D)

        x_in = [sem(f"x_in{b}") for b in range(B)]
        ctx_in_sem = [sem(f"ctx_in{b}") for b in range(B)]
        w_in = {n: sem(f"{n}_in") for n in ("mask", "wmem", "wgate", "bgate", "normw", "lncol", "gates", "wkv",
                                            "wq", "wo", "w1", "w2")}
        const_ready = sem("const_ready")
        flag_ready = sem("flag_ready")
        flag_step = sem("flag_step")
        pool_step = sem("pool_step")
        gates_ready = sem("gates_ready")
        out_done = sem("out_done")
        pe = {k: sem(f"pe_{k}") for k in ("xT", "ctxT", "gatew", "gatem", "qbias", "hbias", "y", "scores", "spread",
                                          "u", "gate", "xhT", "k", "v", "q", "av", "wo", "h2T", "ff1", "ff2")}
        act = {k: sem(f"act_{k}") for k in ("xT", "y", "exp", "spread", "u", "tanh", "square", "xhT", "k", "v", "o",
                                            "h2T", "gelu", "geluhi", "wsplit", "gatew")}
        dve = {k: sem(f"dve_{k}") for k in ("ctxT", "gatew", "gatem", "qbias", "hbias", "negmax", "rcp", "spread",
                                            "gated", "ms", "ve", "xhat", "xhT", "k", "v", "q", "o", "wo",
                                            "ve2", "x2hat", "h2T", "gelu", "out", "wsplit", "mask")}
        pool = {k: sem(f"pool_{k}") for k in ("rms", "rstd", "probs", "rstd2", "wsplit")}

        PRO = list(prologue())
        plans = {nt: PRO + list(body(nt)) for nt in (1, KT)}

        def counts(nt):
            seen, place = {}, {}
            for st in plans[nt]:
                seen[st[0]] = seen.get(st[0], 0) + 1
                place[st] = seen[st[0]]
            return place

        class Path:

            def __init__(self, nt):
                self.nt = nt
                self.plan = plans[nt]
                self.at = counts(nt)
                self.units = 4 * nt
                self.heads = 4 // nt
                self.general = []
                for st in self.plan:
                    n = {"xT": 1, "ctxT": 1, "weights": 4, "qbias": 1, "y": 1, "u": 1, "gate": 2, "xhT": 1, "k": 1,
                         "v": 1, "q": 1, "w1load": 1, "wo": 1, "h2T": 1, "ff1": 1, "ff2": 1}.get(st[0], 0)
                    self.general += [(st, i) for i in range(n)]
                self.use = {key: n for n, key in enumerate(self.general)}

            def bank(self, st, i=0):
                return GEN[self.use[(st, i)] % len(GEN)]

            def bank_free(self, st, i=0):
                n = self.use[(st, i)] - len(GEN)
                if n < 0:
                    return []
                old, j = self.general[n]
                c = self.at[old]
                return {
                    "xT": [(act["xT"], c)], "ctxT": [(dve["ctxT"], c)],
                    "weights": [[(dve["gatew"], 1)], [(dve["gatew"], 2)], [(act["gatew"], 1)],
                                [(dve["gatem"], 1)]][j] if old[0] == "weights" else None,
                    "qbias": [(dve["qbias"], 1)], "w1load": [(dve["hbias"], 1)],
                    "y": [(act["y"], c)], "u": [(act["u"], c)], "gate": [(dve["gated"], T * (c - 1) + j + 1)],
                    "xhT": [(dve["xhT"], c)], "k": [(dve["k"], c), (act["k"], c)],
                    "v": [(act["v"], (c + 1) // 2)] if c % 2 else [(dve["v"], c // 2)],
                    "q": [(dve["q"], c)], "wo": [(dve["wo"], c)], "h2T": [(dve["h2T"], c)],
                    "ff1": [(act["gelu"], c)], "ff2": [(dve["out"], c)],
                }[old[0]]

            def score_no(self, kind, b, u, t):
                return T * (self.at[("scores", kind, b, u)] - 1) + t

            def last_unit(self, pair):
                return (2 * pair + 1) // self.heads

            def quads(self, b, u):
                return 4 * b + (u + 1) // self.nt

        paths = {nt: Path(nt) for nt in (1, KT)}

        def split_matmul(bank_ap, lhs, rhs, start, stop):
            for n, (a, c) in enumerate(((HI, HI), (HI, LO), (LO, HI))):
                last = nc.tensor.matmul(bank_ap, lhs(a), rhs(c), start=start and n == 0, stop=stop and n == 2)
            return last

        def spread_to(eng, path, st, t):
            kind, b, u = st[1:]
            if kind == "ctx":
                if b:
                    eng.wait_ge(pe["u"], b)
                return ctx_probsT[:, :, t * P:(t + 1) * P]
            unit = b * path.units + u
            if unit >= 2:
                eng.wait_ge(pe["av"], unit - 1)
            return probsT[:, unit % 2, :, t * P:(t + 1) * P]

        block = stack.enter_context(nc.Block())

        @block.sync
        def _(sp):
            def load(dst, src, s):
                sp.dma_start(dst, src).then_inc(s, 16)

            def load_x(b):
                load(x_sb[:, b * T:(b + 1) * T, :], x[b].rearrange("(t p) d -> p t d", p=P), x_in[b])

            def load_ctx(b):
                load(ctx_sb[:, b * KT:(b + 1) * KT, :], ctx_in[b].rearrange("(t p) e -> p t e", p=P), ctx_in_sem[b])

            load_x(0)
            load_ctx(0)
            load(wmem_sb[:, :, :], w_mem.rearrange("(p k) e -> p k e", k=K), w_in["wmem"])
            load(wgate_sb[:, :, :], w_gate.rearrange("(k p) f -> p k f", p=P), w_in["wgate"])
            load(mask_u8[:, :], mask.rearrange("(a b) m -> a (b m)", a=1), w_in["mask"])
            load(bgate_row[:, :], b_gate.rearrange("(a d) -> a d", a=1), w_in["bgate"])
            load(stage[:, :].rearrange("p (k n) -> p k n", k=K), wq.rearrange("(p k) n -> p k n", k=K), w_in["wq"])
            for b in range(1, B):
                load_ctx(b)
            load(wkv_sb[:, :], wkv, w_in["wkv"])
            for b in range(1, B):
                load_x(b)
            sp.wait_ge(act["wsplit"], 1)
            sp.wait_ge(dve["wsplit"], 1)
            sp.wait_ge(pe["qbias"], 1)
            load(stage[:, :].rearrange("p (i n) -> p i n", n=D), wo.rearrange("(i p) n -> p i n", p=P), w_in["wo"])
            sp.wait_ge(act["wsplit"], 2)
            sp.wait_ge(pool["wsplit"], 1)
            load(stage[:, :].rearrange("p (k n) -> p k n", k=K), w1.rearrange("(p k) n -> p k n", k=K), w_in["w1"])
            sp.wait_ge(act["wsplit"], 3)
            sp.wait_ge(dve["wsplit"], 2)
            sp.wait_ge(pe["hbias"], 1)
            load(stage[:, :].rearrange("p (i n) -> p i n", n=D), w2.rearrange("(i p) n -> p i n", p=P), w_in["w2"])
            for b in range(B):
                for t in range(T):
                    sp.wait_ge(dve["out"], b * T + t + 1)
                    sp.dma_start(out[b, t * P:(t + 1) * P, :], x_sb[:, b * T + t, :]).then_inc(out_done, 16)
            sp.wait_ge(out_done, 16 * B * T)

        @block.gpsimd
        def _(gp):
            with nc.allow_non_contiguous_dma(reason="single values"):
                gp.dma_start(gates[:, 0:1], attn_gate.rearrange("(a c) -> a c", a=1).to_broadcast([P, 1])
                             ).then_inc(w_in["gates"], 16)
                gp.dma_start(gates[:, 1:2], ff_gate.rearrange("(a c) -> a c", a=1).to_broadcast([P, 1])
                             ).then_inc(w_in["gates"], 16)
            gp.dma_start(normw_sb[:, :], norm_w.rearrange("(a d) -> a d", a=1).to_broadcast([P, D])
                         ).then_inc(w_in["normw"], 16)
            for i, v in enumerate((lnq_g, lnq_b, lnf_g, lnf_b)):
                gp.dma_start(lncol[:, i, :], v.rearrange("(p k) -> p k", k=K)).then_inc(w_in["lncol"], 16)
            nc.gpsimd.memset(ident[:, :], 0.0).then_inc(pool_step, 1)
            nc.gpsimd.memset(ones_row[:, :], 1.0).then_inc(const_ready, 1)
            nc.gpsimd.memset(ones_bf[:, :], 1.0).then_inc(const_ready, 1)
            gp.wait_ge(pool_step, 1)
            nc.gpsimd.affine_select(out=ident[:, :], in_=ident[:, :], compare_op=ALU.not_equal, fill=1.0, base=0,
                                    pattern=[[-1, P]], channel_multiplier=1).then_inc(const_ready, 1)
            nc.gpsimd.memset(half_pow[:, :], -0.5).then_inc(const_ready, 1)
            nc.gpsimd.memset(k_split[0:DH, :, :, 1, :], 0.0).then_inc(const_ready, 1)
            gp.wait_ge(const_ready, 5)
            nc.gpsimd.memset(k_split[DH:P, :, :, 0, :], 0.0).then_inc(const_ready, 1)

            def run(path, plan):
                for st in plan:
                    c = path.at[st]
                    if st[0] == "norm":
                        for t in range(T):
                            n = path.score_no(*st[1:], t)
                            r, hb = n % RING, (path.heads if st[1] == "head" else 1)
                            gp.wait_ge(dve["rcp"], n + 1)
                            if n >= RING:
                                gp.wait_ge(pe["spread"], n - RING + 1)
                            nc.gpsimd.tensor_tensor(
                                probs[:, r, :].rearrange("p (h k) -> p h k", h=hb),
                                expd[:, r, :].rearrange("p (h k) -> p h k", h=hb),
                                row_rcp[:, r, 0:hb].rearrange("p (h k) -> p h k", k=1).to_broadcast([P, hb, BANK // hb]),
                                ALU.mult).then_inc(pool["probs"], 1)
                    elif st[0] == "rms":
                        gp.wait_ge(dve["ms"], c)
                        if c > 1:
                            gp.wait_ge(dve["ve"], c - 1)
                        nc.gpsimd.tensor_tensor(rms_r[:, :], ms[:, :], half_pow[:, :], ALU.pow).then_inc(pool["rms"], 1)
                    elif st[0] == "ln1":
                        gp.wait_ge(dve["ve"], c)
                        if c > 1:
                            gp.wait_ge(dve["xhat"], c - 1)
                        nc.gpsimd.tensor_tensor(rstd[:, :], ve[:, :], half_pow[:, :], ALU.pow).then_inc(pool["rstd"], 1)
                    elif st[0] == "ln2":
                        gp.wait_ge(dve["ve2"], c)
                        nc.gpsimd.tensor_tensor(rstd2[:, st[1], :], ve2[:, st[1], :], half_pow[:, :], ALU.pow
                                                ).then_inc(pool["rstd2"], 1)
                    elif st[0] == "splito":
                        gp.wait_ge(act["wsplit"], 2)
                        nc.gpsimd.tensor_tensor(wo_pair[:, LO, :], stage[:, :], wo_pair[:, HI, :].bitcast(F32),
                                                ALU.subtract).then_inc(pool["wsplit"], 1)

            gp.wait_ge(const_ready, 6)
            run(paths[1], PRO)
            gp.wait_ge(flag_ready, 1)
            short = gp.value_load(short_flag[0:1, 0:1], min_val=0, max_val=1)
            with gp.If(short == 1):
                run(paths[1], paths[1].plan[len(PRO):])
            with gp.Else():
                run(paths[KT], paths[KT].plan[len(PRO):])

        @block.scalar
        def _(sc):
            def run(path, plan):
                for st in plan:
                    kind, c = st[0], path.at[st]
                    if kind == "xT":
                        b = st[1]
                        sc.wait_ge(pe["xT"], c)
                        if b:
                            sc.wait_ge(pe["gate"], T * b)
                        nc.scalar.copy(xT, path.bank(st)[:, :].rearrange("p (k n) -> p k n", k=K)
                                       ).then_inc(act["xT"], 1)
                    elif kind == "weights":
                        sc.wait_ge(pe["gatew"], 3)
                        nc.scalar.copy(gate_mem[:, D:2 * D].rearrange("e (p k) -> e k p", k=K),
                                       path.bank(st, 2)[:, 0:D].rearrange("e (k p) -> e k p", k=K)
                                       ).then_inc(act["gatew"], 1)
                        sc.wait_ge(w_in["gates"], 32)
                        nc.scalar.activation(gates[:, 2:4], gates[:, 0:2], ACT.Tanh).then_inc(gates_ready, 1)
                    elif kind == "y":
                        sc.wait_ge(pe["y"], c)
                        if c > 1:
                            sc.wait_ge(pe["scores"], path.score_no("ctx", st[1] - 1, 0, T - 1) + 1)
                        nc.scalar.activation(yT, path.bank(st)[:, 0:N], ACT.Copy, scale=D ** -0.5
                                             ).then_inc(act["y"], 1)
                    elif kind == "scores":
                        for t in range(T):
                            n = path.score_no(*st[1:], t)
                            r, hb = n % RING, (path.heads if st[1] == "head" else 1)
                            sc.wait_ge(dve["negmax"], n + 1)
                            if n >= RING:
                                sc.wait_ge(pool["probs"], n - RING + 1)
                            w = BANK // hb
                            for h in range(hb):
                                last = nc.scalar.activation(
                                    expd[:, r, h * w:(h + 1) * w], SC[n % 2][:, h * w:(h + 1) * w], ACT.Exp,
                                    bias=neg_max[:, r, h:h + 1], accum_out=row_sum[:, r, h:h + 1])
                            last.then_inc(act["exp"], 1)
                    elif kind == "spread":
                        n = path.score_no(*st[1:], 0)
                        sc.wait_ge(pe["spread"], n + 1)
                        nc.scalar.copy(spread_to(sc, path, st, 0),
                                       SPREAD[n % 2][:, :].rearrange("p (j n) -> p j n", j=4)
                                       ).then_inc(act["spread"], 1)
                    elif kind == "u":
                        sc.wait_ge(pe["u"], c)
                        if c > 1:
                            sc.wait_ge(pe["gate"], T * (c - 1))
                        nc.scalar.copy(uT, path.bank(st)[:, 0:N]).then_inc(act["u"], 1)
                    elif kind == "gate":
                        for t in range(T):
                            sc.wait_ge(pe["gate"], T * (c - 1) + t + 1)
                            if c > 1:
                                sc.wait_ge(act["square"], c - 1)
                            nc.scalar.activation(th[:, t, :], path.bank(st, t)[:, 0:D], ACT.Tanh, scale=0.5
                                                 ).then_inc(act["tanh"], 1)
                    elif kind == "fuse":
                        for t in range(T):
                            sc.wait_ge(dve["gated"], T * (c - 1) + t + 1)
                            last = nc.scalar.activation(th[:, t, :], fused[:, t, :], ACT.Square,
                                                        accum_out=sumsq[:, t:t + 1])
                        last.then_inc(act["square"], 1)
                    elif kind == "xhT":
                        sc.wait_ge(pe["xhT"], c)
                        if c > 1:
                            sc.wait_ge(pe["q"], path.at[("q", st[1] - 1, 3)])
                        nc.scalar.copy(xhT_pair[:, HI, :, :], path.bank(st)[:, :].rearrange("p (k n) -> p k n", k=K)
                                       ).then_inc(act["xhT"], 1)
                    elif kind == "k":
                        sc.wait_ge(pe["k"], c)
                        nc.scalar.copy(k_split[0:DH, st[2], :, 0, :],
                                       path.bank(st)[0:DH, :].rearrange("p (s n) -> p s n", s=KT)
                                       ).then_inc(act["k"], 1)
                    elif kind == "v" and st[3] == 0:
                        sc.wait_ge(pe["v"], c)
                        nc.scalar.copy(v_sb[:, st[2], 0:BANK], path.bank(st)[:, :]).then_inc(act["v"], 1)
                    elif kind == "av":
                        b, u = st[1:]
                        if (u + 1) % path.nt == 0:
                            g = path.quads(b, u)
                            sc.wait_ge(pe["av"], c)
                            if b:
                                sc.wait_ge(pe["wo"], b)
                            j = (u // path.nt) * 2
                            nc.scalar.copy(oT_pair[:, HI, j:j + 2, :],
                                           CONTEXT[:, :].rearrange("p (j n) -> p j n", j=2)).then_inc(act["o"], 1)
                    elif kind == "splitq":
                        sc.wait_ge(w_in["wq"], 16)
                        sc.wait_ge(dve["mask"], 2)
                        for k in range(K):
                            last = nc.scalar.activation(wq_p[:, HI, k, :], wq_raw[:, k, :], ACT.Copy,
                                                        scale=q_scale[:, k:k + 1])
                        last.then_inc(act["wsplit"], 1)
                    elif kind == "splito":
                        sc.wait_ge(w_in["wo"], 16)
                        nc.scalar.copy(wo_pair[:, HI, :], stage[:, :]).then_inc(act["wsplit"], 1)
                    elif kind == "split1":
                        sc.wait_ge(w_in["w1"], 16)
                        sc.wait_ge(pe["q"], path.at[("q", B - 1, 3)])
                        for k in range(K):
                            last = nc.scalar.activation(w1_p[:, HI, k, :], wq_raw[:, k, :], ACT.Copy,
                                                        scale=lncol[:, 2, k:k + 1])
                        last.then_inc(act["wsplit"], 1)
                    elif kind == "split2":
                        sc.wait_ge(w_in["w2"], 16)
                        sc.wait_ge(pe["av"], path.at[("av", B - 1, path.units - 1)])
                        nc.scalar.copy(w2_pair[:, HI, :, :], stage[:, :].rearrange("p (i n) -> p i n", n=D)
                                       ).then_inc(act["wsplit"], 1)
                    elif kind == "h2T":
                        f, half = st[1:]
                        sc.wait_ge(pe["h2T"], c)
                        if f:
                            sc.wait_ge(pe["ff1"], FM * f)
                        nc.scalar.copy(h2T_pair[:, HI, :, half * N:(half + 1) * N],
                                       path.bank(st)[:, :].rearrange("p (k n) -> p k n", k=K)
                                       ).then_inc(act["h2T"], 1)
                    elif kind == "ff1":
                        f, m = st[1:]
                        sc.wait_ge(pe["ff1"], c)
                        if c == 1:
                            sc.wait_ge(dve["hbias"], 1)
                        if c > RING:
                            sc.wait_ge(dve["gelu"], c - RING)
                        nc.scalar.activation(expd[:, (c - 1) % RING, :], path.bank(st)[:, :], ACT.Gelu,
                                             bias=h_bias[:, m:m + 1]).then_inc(act["gelu"], 1)
                        if f:
                            sc.wait_ge(pe["ff2"], 2 * T * f)
                        sc.wait_ge(act["gelu"], c)
                        nc.scalar.copy(gelu_pair[:, HI, m, :], expd[:, (c - 1) % RING, :]).then_inc(act["geluhi"], 1)

            run(paths[1], PRO)
            sc.wait_ge(flag_ready, 1)
            short = sc.value_load(short_flag[0:1, 0:1], min_val=0, max_val=1)
            with sc.If(short == 1):
                run(paths[1], paths[1].plan[len(PRO):])
            with sc.Else():
                run(paths[KT], paths[KT].plan[len(PRO):])

        @block.vector
        def _(ve_):
            def chain(ins):
                flag_count[0] += 1
                ins.then_inc(flag_step, 1)
                ve_.wait_ge(flag_step, flag_count[0])

            flag_count = [0]

            def norm_stats(tiles, dst, b_tiles):
                for i, t in enumerate(tiles):
                    last = nc.vector.bn_stats(stats[:, i, :], x_sb[:, t, :])
                chain(last)
                for i, t in enumerate(tiles):
                    last = nc.vector.bn_aggr(dst[:, b_tiles + i, :], stats[:, i, :])
                chain(last)

            def run(path, plan):
                for st in plan:
                    kind, c = st[0], path.at[st]
                    if kind == "ctxT":
                        ve_.wait_ge(pe["ctxT"], c)
                        nc.vector.tensor_copy(ctxT[:, st[1], :], path.bank(st)[:, :]).then_inc(dve["ctxT"], 1)
                    elif kind == "weights":
                        for i, dst in enumerate((gate_xT, gate_cT)):
                            ve_.wait_ge(pe["gatew"], i + 1)
                            nc.vector.tensor_copy(dst[:, :, :], path.bank(st, i)[:, :].rearrange("p (k n) -> p k n", k=K)
                                                  ).then_inc(dve["gatew"], 1)
                        ve_.wait_ge(pe["gatem"], 1)
                        nc.vector.tensor_copy(gate_mem[:, 0:D], path.bank(st, 3)[:, 0:D]).then_inc(dve["gatem"], 1)
                    elif kind == "qbias":
                        ve_.wait_ge(pe["qbias"], 1)
                        nc.vector.tensor_scalar(q_bias[:, :], path.bank(st)[:, 0:PAIRS], DH ** -0.5, None, ALU.mult
                                                ).then_inc(dve["qbias"], 1)
                    elif kind == "w1load":
                        ve_.wait_ge(pe["hbias"], 1)
                        nc.vector.tensor_copy(h_bias[:, :], path.bank(st)[:, 0:FM]).then_inc(dve["hbias"], 1)
                    elif kind == "scores":
                        for t in range(T):
                            n = path.score_no(*st[1:], t)
                            r, hb = n % RING, (path.heads if st[1] == "head" else 1)
                            ve_.wait_ge(pe["scores"], n + 1)
                            nc.vector.tensor_reduce(neg_max[:, r, 0:hb],
                                                    SC[n % 2][:, :].rearrange("p (h k) -> p h k", h=hb),
                                                    AX_X, ALU.max, negate=True).then_inc(dve["negmax"], 1)
                    elif kind == "norm":
                        for t in range(T):
                            n = path.score_no(*st[1:], t)
                            r, hb = n % RING, (path.heads if st[1] == "head" else 1)
                            ve_.wait_ge(act["exp"], n + 1)
                            nc.vector.reciprocal(row_rcp[:, r, 0:hb], row_sum[:, r, 0:hb]).then_inc(dve["rcp"], 1)
                    elif kind == "spread":
                        n = path.score_no(*st[1:], 1)
                        ve_.wait_ge(pe["spread"], n + 1)
                        nc.vector.tensor_copy(spread_to(ve_, path, st, 1),
                                              SPREAD[n % 2][:, :].rearrange("p (j n) -> p j n", j=4)
                                              ).then_inc(dve["spread"], 1)
                    elif kind == "gate":
                        for t in range(T):
                            ve_.wait_ge(act["tanh"], T * (c - 1) + t + 1)
                            if c > 1:
                                ve_.wait_ge(act["square"], c - 1)
                            chain(nc.vector.scalar_tensor_tensor(
                                fused[:, t, :], th[:, t, :], 1.0, path.bank(st, t)[:, D:2 * D], ALU.add, ALU.mult))
                            gated = nc.vector.scalar_tensor_tensor(
                                fused[:, t, :], fused[:, t, :], 0.5, x_sb[:, st[1] * T + t, :], ALU.mult, ALU.add)
                            gated.then_inc(dve["gated"], 1)
                    elif kind == "rms":
                        ve_.wait_ge(act["square"], c)
                        nc.vector.tensor_scalar(ms[:, :], sumsq[:, :], 1.0 / D, RMS_EPS, ALU.mult, ALU.add
                                                ).then_inc(dve["ms"], 1)
                    elif kind == "ln1":
                        b = st[1]
                        ve_.wait_ge(pool["rms"], c)
                        if c == 1:
                            ve_.wait_ge(w_in["normw"], 16)
                        for t in range(T):
                            last = nc.vector.scalar_tensor_tensor(
                                x_sb[:, b * T + t, :], fused[:, t, :], rms_r[:, t:t + 1], normw_sb[:, :],
                                ALU.mult, ALU.mult)
                        chain(last)
                        norm_stats(range(b * T, b * T + T), mean_var, 0)
                        nc.vector.tensor_scalar(ve[:, :], mean_var[:, :, 1], LN_EPS, None, ALU.add
                                                ).then_inc(dve["ve"], 1)
                    elif kind == "xhat":
                        b = st[1]
                        ve_.wait_ge(pool["rstd"], c)
                        if c > 1:
                            ve_.wait_ge(pe["xhT"], c - 1)
                        for t in range(T):
                            last = nc.vector.tensor_scalar(xhat[:, t, :], x_sb[:, b * T + t, :], mean_var[:, t, 0:1],
                                                           rstd[:, t:t + 1], ALU.subtract, ALU.mult)
                        last.then_inc(dve["xhat"], 1)
                    elif kind == "xhT":
                        ve_.wait_ge(act["xhT"], c)
                        nc.vector.tensor_tensor(xhT_pair[:, LO, :, :],
                                                path.bank(st)[:, :].rearrange("p (k n) -> p k n", k=K),
                                                xhT_pair[:, HI, :, :].bitcast(F32), ALU.subtract
                                                ).then_inc(dve["xhT"], 1)
                    elif kind == "k":
                        ve_.wait_ge(pe["k"], c)
                        nc.vector.tensor_copy(k_split[DH:P, st[2], :, 1, :],
                                              path.bank(st)[DH:P, :].rearrange("p (s n) -> p s n", s=KT)
                                              ).then_inc(dve["k"], 1)
                    elif kind == "v" and st[3] == 1:
                        ve_.wait_ge(pe["v"], c)
                        nc.vector.tensor_copy(v_sb[:, st[2], BANK:2 * BANK], path.bank(st)[:, :]).then_inc(dve["v"], 1)
                    elif kind == "q":
                        b, j = st[1:]
                        ve_.wait_ge(pe["q"], c)
                        if c == 1:
                            ve_.wait_ge(dve["qbias"], 1)
                        if b:
                            ve_.wait_ge(pe["scores"],
                                        path.score_no("head", b - 1, path.last_unit(2 * j + 1), T - 1) + 1)
                        for i in range(2):
                            pair = 2 * j + i
                            last = nc.vector.tensor_scalar(q_sb[:, pair, :], path.bank(st)[:, i * N:(i + 1) * N],
                                                           q_bias[:, pair:pair + 1], None, ALU.add)
                        last.then_inc(dve["q"], 1)
                    elif kind == "av":
                        b, u = st[1:]
                        if (u + 1) % path.nt == 0:
                            g = path.quads(b, u)
                            ve_.wait_ge(act["o"], g)
                            j = (u // path.nt) * 2
                            nc.vector.tensor_tensor(oT_pair[:, LO, j:j + 2, :],
                                                    CONTEXT[:, :].rearrange("p (j n) -> p j n", j=2),
                                                    oT_pair[:, HI, j:j + 2, :].bitcast(F32), ALU.subtract
                                                    ).then_inc(dve["o"], 1)
                    elif kind == "splitq":
                        ve_.wait_ge(act["wsplit"], 1)
                        for k in range(K):
                            last = nc.vector.scalar_tensor_tensor(
                                wq_p[:, LO, k, :], wq_raw[:, k, :], q_scale[:, k:k + 1],
                                wq_p[:, HI, k, :].bitcast(F32), ALU.mult, ALU.subtract)
                        last.then_inc(dve["wsplit"], 1)
                    elif kind == "split1":
                        ve_.wait_ge(act["wsplit"], 3)
                        for k in range(K):
                            last = nc.vector.scalar_tensor_tensor(
                                w1_p[:, LO, k, :], wq_raw[:, k, :], lncol[:, 2, k:k + 1],
                                w1_p[:, HI, k, :].bitcast(F32), ALU.mult, ALU.subtract)
                        last.then_inc(dve["wsplit"], 1)
                    elif kind == "split2":
                        ve_.wait_ge(act["wsplit"], 4)
                        nc.vector.tensor_tensor(w2_pair[:, LO, :, :], stage[:, :].rearrange("p (i n) -> p i n", n=D),
                                                w2_pair[:, HI, :, :].bitcast(F32), ALU.subtract
                                                ).then_inc(dve["wsplit"], 1)
                    elif kind == "wo":
                        b = st[1]
                        ve_.wait_ge(pe["wo"], c)
                        if c == 1:
                            ve_.wait_ge(gates_ready, 1)
                        nc.vector.scalar_tensor_tensor(
                            x_sb[:, b * T:b * T + T, :], path.bank(st)[:, :].rearrange("p (t n) -> p t n", t=T),
                            gates[:, 2:3], x_sb[:, b * T:b * T + T, :], ALU.mult, ALU.add).then_inc(dve["wo"], 1)
                    elif kind == "ln2":
                        b = st[1]
                        ve_.wait_ge(dve["wo"], path.at[("wo", b)])
                        norm_stats(range(b * T, b * T + T), mean_var2, b * T)
                        nc.vector.tensor_scalar(ve2[:, b, :], mean_var2[:, b * T:b * T + T, 1], LN_EPS, None, ALU.add
                                                ).then_inc(dve["ve2"], 1)
                    elif kind == "x2hat":
                        b = st[1]
                        ve_.wait_ge(pool["rstd2"], path.at[("ln2", b)])
                        if c == 1:
                            ve_.wait_ge(pe["xhT"], B)
                        else:
                            ve_.wait_ge(pe["h2T"], c - 1)
                        for t in range(T):
                            last = nc.vector.tensor_scalar(xhat[:, t, :], x_sb[:, b * T + t, :],
                                                           mean_var2[:, b * T + t, 0:1], rstd2[:, b, t:t + 1],
                                                           ALU.subtract, ALU.mult)
                        last.then_inc(dve["x2hat"], 1)
                    elif kind == "h2T":
                        f, half = st[1:]
                        ve_.wait_ge(act["h2T"], c)
                        nc.vector.tensor_tensor(h2T_pair[:, LO, :, half * N:(half + 1) * N],
                                                path.bank(st)[:, :].rearrange("p (k n) -> p k n", k=K),
                                                h2T_pair[:, HI, :, half * N:(half + 1) * N].bitcast(F32),
                                                ALU.subtract).then_inc(dve["h2T"], 1)
                    elif kind == "ff1":
                        f, m = st[1:]
                        ve_.wait_ge(act["geluhi"], c)
                        nc.vector.tensor_tensor(gelu_pair[:, LO, m, :], expd[:, (c - 1) % RING, :],
                                                gelu_pair[:, HI, m, :].bitcast(F32), ALU.subtract
                                                ).then_inc(dve["gelu"], 1)
                    elif kind == "ff2":
                        f, i = st[1:]
                        tile = 2 * T * f + i
                        ve_.wait_ge(pe["ff2"], c)
                        nc.vector.scalar_tensor_tensor(
                            x_sb[:, tile, :], path.bank(st)[:, 0:D], gates[:, 3:4], x_sb[:, tile, :],
                            ALU.mult, ALU.add).then_inc(dve["out"], 1)

            ve_.wait_ge(w_in["mask"], 16)
            nc.vector.tensor_scalar(mask_bias[:, :], mask_u8[:, :], 1.0, -MASKED, ALU.subtract, ALU.mult
                                    ).then_inc(dve["mask"], 1)
            chain(nc.vector.reduce_max(tile_any[:, :], mask_u8[:, :].rearrange("a (t n) -> a t n", n=P), AX_X))
            any_v = tile_any[:, :].rearrange("a (b t) -> a b t", t=KT)
            chain(nc.vector.reduce_max(flag_work[:, 0:B], any_v[:, :, 0:HOT], AX_X))
            chain(nc.vector.tensor_scalar(flag_work[:, B:2 * B], flag_work[:, 0:B], -1.0, 1.0, ALU.mult, ALU.add))
            chain(nc.vector.tensor_tensor(flag_work[:, 2 * B:3 * B], flag_work[:, B:2 * B], any_v[:, :, HOT], ALU.mult))
            nc.vector.tensor_reduce(short_flag[:, :], flag_work[:, 2 * B:3 * B], AX_X, ALU.min).then_inc(flag_ready, 1)
            ve_.wait_ge(w_in["lncol"], 64)
            nc.vector.tensor_scalar(q_scale[:, :], lncol[:, 0, :], DH ** -0.5, None, ALU.mult).then_inc(dve["mask"], 1)
            ve_.wait_ge(dve["mask"], 2)
            run(paths[1], PRO)
            before = flag_count[0]
            ve_.wait_ge(flag_ready, 1)
            short = ve_.value_load(short_flag[0:1, 0:1], min_val=0, max_val=1)
            with ve_.If(short == 1):
                run(paths[1], paths[1].plan[len(PRO):])
            with ve_.Else():
                flag_count[0] = before
                run(paths[KT], paths[KT].plan[len(PRO):])

        @block.tensor
        def _(te):
            def free(path, st, i=0):
                for s, v in path.bank_free(st, i):
                    te.wait_ge(s, v)

            def run(path, plan):
                for st in plan:
                    kind, c = st[0], path.at[st]
                    if kind == "xT":
                        b = st[1]
                        te.wait_ge(x_in[b], 16)
                        free(path, st)
                        for k in range(K):
                            for t in range(T):
                                last = nc.tensor.transpose(path.bank(st)[:, k * N + t * P:k * N + (t + 1) * P],
                                                           x_sb[:, b * T + t, k:D:K], ident[:, :])
                        last.then_inc(pe["xT"], 1)
                    elif kind == "ctxT":
                        b = st[1]
                        te.wait_ge(ctx_in_sem[b], 16)
                        free(path, st)
                        for j in range(KT):
                            last = nc.tensor.transpose(path.bank(st)[:, j * P:(j + 1) * P], ctx_sb[:, b * KT + j, :],
                                                       ident[:, :])
                        last.then_inc(pe["ctxT"], 1)
                    elif kind == "weights":
                        te.wait_ge(w_in["wgate"], 16)
                        for i in range(2):
                            free(path, st, i)
                            for k in range(K):
                                for dt in range(K):
                                    last = nc.tensor.transpose(
                                        path.bank(st, i)[:, k * D + dt * P:k * D + (dt + 1) * P],
                                        wgate_sb[:, dt, i * D + k:(i + 1) * D:K], ident[:, :])
                            last.then_inc(pe["gatew"], 1)
                        te.wait_ge(w_in["wmem"], 16)
                        free(path, st, 2)
                        for k in range(K):
                            last = nc.tensor.transpose(path.bank(st, 2)[:, k * P:(k + 1) * P], wmem_sb[:, k, :],
                                                       ident[:, :])
                        last.then_inc(pe["gatew"], 1)
                        te.wait_ge(dve["gatew"], 2)
                        free(path, st, 3)
                        for k in range(K):
                            last = nc.tensor.matmul(path.bank(st, 3)[:, 0:D], wmem_sb[:, k, :], gate_cT[:, k, :],
                                                    start=k == 0, stop=k == K - 1)
                        last.then_inc(pe["gatem"], 1)
                    elif kind in ("qbias", "w1load"):
                        if kind == "qbias":
                            te.wait_ge(w_in["wq"], 16)
                            te.wait_ge(w_in["lncol"], 64)
                        else:
                            te.wait_ge(w_in["w1"], 16)
                        free(path, st)
                        shift = lncol[:, 1 if kind == "qbias" else 3, :]
                        for m in range(PAIRS):
                            for k in range(K):
                                last = nc.tensor.matmul(path.bank(st)[:, m:m + 1], wq_raw[:, k, m * P:(m + 1) * P],
                                                        shift[:, k:k + 1], start=k == 0, stop=k == K - 1)
                        last.then_inc(pe["qbias" if kind == "qbias" else "hbias"], 1)
                    elif kind == "y":
                        te.wait_ge(act["xT"], c)
                        free(path, st)
                        for k in range(K):
                            last = nc.tensor.matmul(path.bank(st)[:, 0:N], wmem_sb[:, k, :], xT[:, k, :],
                                                    start=k == 0, stop=k == K - 1)
                        last.then_inc(pe["y"], 1)
                    elif kind == "scores":
                        what, b, u = st[1:]
                        for t in range(T):
                            n = path.score_no(what, b, u, t)
                            if n >= 2:
                                te.wait_ge(act["exp"], n - 1)
                            toks = slice(t * P, (t + 1) * P)
                            if what == "ctx":
                                if t == 0:
                                    te.wait_ge(act["y"], path.at[("y", b)])
                                    te.wait_ge(dve["ctxT"], path.at[("ctxT", b)])
                                last = nc.tensor.matmul(SC[n % 2][:, :], yT[:, toks], ctxT[:, b, :],
                                                        start=True, stop=True)
                            else:
                                if t == 0:
                                    te.wait_ge(dve["q"], path.at[("q", b, (u * path.heads) // 4)])
                                    if u == 0:
                                        cb = b if path.nt > 1 else 0
                                        te.wait_ge(act["k"], path.at[("k", cb, PAIRS - 1)])
                                        te.wait_ge(dve["k"], path.at[("k", cb, PAIRS - 1)])
                                if path.nt == 1:
                                    kept = mask_bias[0:1, b * M + HOT * P:b * M + (HOT + 1) * P]
                                    bias = kept.rearrange("a (h k) -> a h k", h=1).to_broadcast([1, 4, P])
                                    nc.tensor.matmul(SC[n % 2][:, :].rearrange("p (h k) -> p h k", h=4),
                                                     ones_bf[0:1, :], bias, start=True, stop=False)
                                    for i in range(2):
                                        last = nc.tensor.matmul(
                                            SC[n % 2][:, i * 2 * P:(i + 1) * 2 * P], q_sb[:, 2 * u + i, toks],
                                            k_split[:, 2 * u + i, b, :, :], start=False, stop=i == 1)
                                else:
                                    nc.tensor.matmul(SC[n % 2][:, :], ones_bf[0:1, :],
                                                     mask_bias[0:1, b * M:(b + 1) * M], start=True, stop=False)
                                    last = nc.tensor.matmul(
                                        SC[n % 2][:, :].rearrange("p (s k) -> p s k", s=KT), q_sb[:, u // 2, toks],
                                        k_split[:, u // 2, :, u % 2, :], start=False, stop=True)
                            last.then_inc(pe["scores"], 1)
                    elif kind == "spread":
                        for t in range(T):
                            n = path.score_no(*st[1:], t)
                            te.wait_ge(pool["probs"], n + 1)
                            if n >= 2:
                                te.wait_ge((act, dve)[t]["spread"], n // 2)
                            for j in range(4):
                                last = nc.tensor.transpose(SPREAD[n % 2][:, j * P:(j + 1) * P],
                                                           probs[:, n % RING, j * P:(j + 1) * P], ident[:, :])
                            last.then_inc(pe["spread"], 1)
                    elif kind == "u":
                        b = st[1]
                        m = path.at[("spread", "ctx", b, 0)]
                        te.wait_ge(act["spread"], m)
                        te.wait_ge(dve["spread"], m)
                        free(path, st)
                        for j in range(KT):
                            last = nc.tensor.matmul(path.bank(st)[:, 0:N], ctx_sb[:, b * KT + j, :],
                                                    ctx_probsT[:, j, :], start=j == 0, stop=j == KT - 1)
                        last.then_inc(pe["u"], 1)
                    elif kind == "gate":
                        te.wait_ge(act["u"], c)
                        if c == 1:
                            te.wait_ge(dve["gatem"], 1)
                            te.wait_ge(act["gatew"], 1)
                            te.wait_ge(w_in["bgate"], 16)
                        for t in range(T):
                            toks = slice(t * P, (t + 1) * P)
                            free(path, st, t)
                            out_b = path.bank(st, t)
                            nc.tensor.matmul(out_b[:, :], uT[:, toks], gate_mem[:, :], start=True, stop=False)
                            nc.tensor.matmul(out_b[:, 0:D], ones_row[0:1, :], bgate_row[0:1, :], start=False,
                                             stop=False)
                            for k in range(K):
                                last = nc.tensor.matmul(out_b[:, 0:D], xT[:, k, toks], gate_xT[:, k, :],
                                                        start=False, stop=k == K - 1)
                            last.then_inc(pe["gate"], 1)
                    elif kind in ("xhT", "h2T"):
                        te.wait_ge(dve["xhat" if kind == "xhT" else "x2hat"], c)
                        free(path, st)
                        for k in range(K):
                            for t in range(T):
                                last = nc.tensor.transpose(path.bank(st)[:, k * N + t * P:k * N + (t + 1) * P],
                                                           xhat[:, t, k:D:K], ident[:, :])
                        last.then_inc(pe[kind], 1)
                    elif kind == "k":
                        b, pair = st[1:]
                        if c == 1:
                            te.wait_ge(w_in["wkv"], 16)
                            te.wait_ge(dve["ctxT"], B)
                        free(path, st)
                        keys = ctxT[:, :, HOT * P:M] if path.nt == 1 else ctxT[:, b, :]
                        nc.tensor.matmul(
                            path.bank(st)[:, :].rearrange("p (s n) -> p s n", s=KT) if path.nt == 1
                            else path.bank(st)[:, :],
                            wkv_sb[:, pair * P:(pair + 1) * P], keys, start=True, stop=True).then_inc(pe["k"], 1)
                    elif kind == "v":
                        b, s, h = st[1:]
                        free(path, st)
                        keys = ctxT[:, s, HOT * P:M] if path.nt == 1 else ctxT[:, b, s * P:(s + 1) * P]
                        nc.tensor.matmul(path.bank(st)[:, :], keys,
                                         wkv_sb[:, INNER + h * BANK:INNER + (h + 1) * BANK],
                                         start=True, stop=True).then_inc(pe["v"], 1)
                    elif kind == "q":
                        b, j = st[1:]
                        if j == 0:
                            te.wait_ge(dve["xhT"], path.at[("xhT", b)])
                            if b == 0:
                                te.wait_ge(dve["wsplit"], 1)
                        free(path, st)
                        for i in range(2):
                            pair = slice((2 * j + i) * P, (2 * j + i + 1) * P)
                            for k in range(K):
                                last = split_matmul(path.bank(st)[:, i * N:(i + 1) * N],
                                                    lambda a: wq_p[:, a, k, pair], lambda a: xhT_pair[:, a, k, :],
                                                    k == 0, k == K - 1)
                        last.then_inc(pe["q"], 1)
                    elif kind == "av":
                        b, u = st[1:]
                        m = path.at[("spread", "head", b, u)]
                        unit = b * path.units + u
                        te.wait_ge(act["spread"], m)
                        te.wait_ge(dve["spread"], m)
                        if u == 0:
                            cv = b if path.nt > 1 else 0
                            te.wait_ge(act["v"], KT * (cv + 1))
                            te.wait_ge(dve["v"], KT * (cv + 1))
                        if u % path.nt == 0:
                            done = path.quads(b, u) - (1 if path.nt == 1 else 0)
                            if done:
                                te.wait_ge(dve["o"], done)
                        if path.nt == 1:
                            for h in range(4):
                                head, half = 4 * u + h, h % 2
                                last = nc.tensor.matmul(
                                    CONTEXT[half * DH:(half + 1) * DH, (h // 2) * N:(h // 2 + 1) * N],
                                    v_sb[:, b, head * DH:(head + 1) * DH], probsT[:, unit % 2, h, :],
                                    start=True, stop=True)
                        else:
                            half, col = u % 2, (u % 4) // 2
                            for s in range(KT):
                                last = nc.tensor.matmul(
                                    CONTEXT[half * DH:(half + 1) * DH, col * N:(col + 1) * N],
                                    v_sb[:, s, u * DH:(u + 1) * DH], probsT[:, unit % 2, s, :],
                                    start=s == 0, stop=s == KT - 1)
                        last.then_inc(pe["av"], 1)
                    elif kind == "wo":
                        b = st[1]
                        te.wait_ge(dve["o"], 4 * (b + 1))
                        if b == 0:
                            te.wait_ge(pool["wsplit"], 1)
                        free(path, st)
                        for t in range(T):
                            toks = slice(t * P, (t + 1) * P)
                            for i in range(PAIRS):
                                last = split_matmul(path.bank(st)[:, t * D:(t + 1) * D],
                                                    lambda a: oT_pair[:, a, i, toks], lambda a: wo_p[:, a, i, :],
                                                    i == 0, i == PAIRS - 1)
                        last.then_inc(pe["wo"], 1)
                    elif kind == "ff1":
                        f, m = st[1:]
                        if m == 0:
                            te.wait_ge(dve["h2T"], 2 * (f + 1))
                            if f == 0:
                                te.wait_ge(dve["wsplit"], 2)
                        free(path, st)
                        for k in range(K):
                            last = split_matmul(path.bank(st)[:, :], lambda a: w1_p[:, a, k, m * P:(m + 1) * P],
                                                lambda a: h2T_pair[:, a, k, :], k == 0, k == K - 1)
                        last.then_inc(pe["ff1"], 1)
                    elif kind == "ff2":
                        f, i = st[1:]
                        toks = slice(i * P, (i + 1) * P)
                        if i == 0:
                            te.wait_ge(dve["gelu"], FM * (f + 1))
                            if f == 0:
                                te.wait_ge(dve["wsplit"], 3)
                        free(path, st)
                        for m in range(FM):
                            last = split_matmul(path.bank(st)[:, 0:D], lambda a: gelu_pair[:, a, m, toks],
                                                lambda a: w2_pair[:, a, m, :], m == 0, m == FM - 1)
                        last.then_inc(pe["ff2"], 1)

            te.wait_ge(const_ready, 6)
            run(paths[1], PRO)
            te.wait_ge(flag_ready, 1)
            te.wait_ge(dve["mask"], 1)
            short = te.value_load(short_flag[0:1, 0:1], min_val=0, max_val=1)
            with te.If(short == 1):
                run(paths[1], paths[1].plan[len(PRO):])
            with te.Else():
                run(paths[KT], paths[KT].plan[len(PRO):])


_INS = ['x', 'ctx_1024', 'mask_BxS2_bk0', 'L0_xattn_W_mem', 'L0_xattn_W_gate', 'L0_xattn_b_gate', 'L0_xattn_norm_w',
        'L1_xattn_ln_q_g', 'L1_xattn_ln_q_b', 'L1_xattn_Wq', 'L1_xattn_Wkv', 'L1_xattn_Wo', 'L1_xattn_attn_gate',
        'L1_xattn_ln_ff_g', 'L1_xattn_ln_ff_b', 'L1_xattn_W1', 'L1_xattn_W2', 'L1_xattn_ff_gate']


def kernel(**inputs):
    import numpy as _np
    import concourse.bacc as _bacc
    from concourse import mybir as _mybir
    from concourse.bass_utils import run_bass_kernel_spmd as _run

    nc = _bacc.Bacc("TRN2", target_bir_lowering=False, num_devices=1)
    arrays, args = {}, []
    for name in _INS:
        a = _np.ascontiguousarray(inputs[name])
        arrays[f"in_{name}_dram"] = a
        args.append(nc.dram_tensor(f"in_{name}_dram", a.shape, _mybir.dt.from_np(a.dtype), kind="ExternalInput").ap())
    shape = inputs['x'].shape
    args.append(nc.dram_tensor("out_0_dram", shape, _mybir.dt.float32, kind="ExternalOutput").ap())
    gated_attention_block(nc, *args)
    r = _run(nc, [arrays], core_ids=[0])
    return r.results[0]["out_0_dram"]
```

```python
from contextlib import ExitStack

import concourse.bass as bass
from concourse import mybir

F32 = mybir.dt.float32
F32R = mybir.dt.float32r
BF16 = mybir.dt.bfloat16
U8 = mybir.dt.uint8
I32 = mybir.dt.int32
ALU = mybir.AluOpType
ACT = mybir.ActivationFunctionType
AX_X = mybir.AxisListType.X

P = 128
BANK = 512
HI, LO = 0, 1
MASKED = -(2.0 ** 100)
RMS_EPS = 1e-6
LN_EPS = 1e-5


def gated_attention_block(nc, x, ctx_in, mask, w_mem, w_gate, b_gate, norm_w, lnq_g, lnq_b, wq, wkv, wo,
                          attn_gate, lnf_g, lnf_b, w1, w2, ff_gate, out):
    B, N, D = x.shape
    M, E = ctx_in.shape[1:]
    INNER = wq.shape[1]
    FF = w1.shape[1]
    DH = 64
    H = INNER // DH
    T = N // P
    KT = M // P
    K = D // P
    PAIRS = H // 2
    FM = FF // P
    HOT = KT - 1
    assert (T, KT, K, DH * 2, D, E) == (2, 4, 2, P, 2 * P, P)

    def prologue():
        yield ("xT", 0)
        yield ("y", 0)
        yield ("ctxT", 0)
        yield ("scores", "ctx", 0, 0)
        yield ("exp", "ctx", 0, 0)
        yield ("norm", "ctx", 0, 0)
        yield ("weights",)
        for b in range(1, B):
            yield ("ctxT", b)
        yield ("spread", "ctx", 0, 0)
        yield ("k", "hot", 0)
        yield ("k", "hot", 1)
        yield ("u", 0)
        yield ("k", "hot", 2)
        yield ("k", "hot", 3)
        yield ("gate", 0)
        yield ("fuse", 0)
        yield ("rms", 0)
        yield ("k", "hot", 4)
        yield ("k", "hot", 5)
        yield ("ln1", 0)
        yield ("xT", 1)
        yield ("mask",)
        yield ("k", "hot", 6)
        yield ("k", "hot", 7)
        yield ("splitq",)
        yield ("xhat", 0)
        yield ("y", 1)
        yield ("xhT", 0)
        yield ("scores", "ctx", 1, 0)
        yield ("exp", "ctx", 1, 0)
        yield ("qbias",)
        yield ("q", 0, 0)
        yield ("norm", "ctx", 1, 0)
        for s in range(KT):
            yield ("v", "hot", s, 0)
            yield ("v", "hot", s, 1)
        yield ("splito",)

    def body(nt):
        units = 4 * nt

        def between(b, slot):
            more = b + 1 < B
            if slot == 0:
                before = [("spread", "ctx", b + 1, 0)] if more else [("x2hat", 0)]
                before.append(("q", b, 1))
                after = [("u", b + 1)] if more else [("h2T", 0, 0), ("q", b, 2)]
            elif slot == 1:
                before = [("gate", b + 1)] if more else [("q", b, 3), ("x2hat", 1)]
                after = [("fuse", b + 1), ("q", b, 2), ("rms", b + 1)] if more else [("h2T", 0, 1), ("split1",)]
            elif slot == 2:
                before = [("ln1", b + 1), ("q", b, 3)] if more else [("hbias",)]
                after = [("xhat", b + 1)] if more else []
                if b + 2 < B:
                    after += [("xT", b + 2), ("y", b + 2)]
            else:
                before = [("xhT", b + 1)] if more else []
                after = [("q", b + 1, 0)] if more else []
                if b + 2 < B:
                    after = [("scores", "ctx", b + 2, 0), ("exp", "ctx", b + 2, 0), ("norm", "ctx", b + 2, 0)] + after
            return before, after

        held = None
        owed = None

        def use():
            yield ("av", *held)

        for b in range(B):
            if nt > 1:
                if held:
                    yield ("spread", "head", *held)
                    if owed:
                        yield ("wo", *owed)
                    yield from use()
                    owed, held = (held[0], held[1] // nt), None
                for pair in range(PAIRS):
                    yield ("k", b, pair)
                for s in range(KT):
                    yield ("v", b, s, 0)
                    yield ("v", b, s, 1)
            for u in range(units):
                slot = u // nt
                before, after = between(b, slot) if u % nt == nt - 1 else ([], [])
                if held:
                    yield ("spread", "head", *held)
                yield ("scores", "head", b, u)
                yield ("exp", "head", b, u)
                projected, owed = owed, None
                if projected:
                    yield ("wo", *projected)
                yield from before
                yield ("norm", "head", b, u)
                if held:
                    yield from use()
                    if (held[1] + 1) % nt == 0:
                        owed = (held[0], held[1] // nt)
                if projected and projected[1] == 3:
                    yield ("ln2", projected[0])
                yield from after
                held = (b, u)
        yield ("ff1", 0, 0)
        yield ("spread", "head", *held)
        if owed:
            yield ("wo", *owed)
        yield ("ff1", 0, 1)
        yield from use()
        yield ("ff1", 0, 2)
        yield ("split2",)
        yield ("ff1", 0, 3)
        yield ("wo", B - 1, 3)
        yield ("ln2", B - 1)
        for m in range(4, FM):
            yield ("ff1", 0, m)
        yield ("x2hat", 2)
        yield ("ff2", 0, 0)
        yield ("h2T", 1, 0)
        yield ("x2hat", 3)
        yield ("ff2", 0, 1)
        yield ("h2T", 1, 1)
        for i in range(2, 2 * T):
            yield ("ff2", 0, i)
        for m in range(FM):
            yield ("ff1", 1, m)
        for i in range(2 * T):
            yield ("ff2", 1, i)

    with ExitStack() as stack:
        def sb(name, shape, dt=F32):
            return stack.enter_context(nc.sbuf_tensor(name, shape, dt))

        def sem(name):
            return stack.enter_context(nc.semaphore(name))

        def psum(name, shape):
            return stack.enter_context(nc.psum_tensor(name, shape, F32))

        ident = sb("ident", [P, P])
        ones_row = sb("ones_row", [1, P])
        ones_bf = sb("ones_bf", [1, P], BF16)
        mask_u8 = sb("mask_u8", [1, B * M], U8)
        mask_bias = sb("mask_bias", [1, B * M], BF16)
        tile_any = sb("tile_any", [1, B * KT])
        flag_work = sb("flag_work", [1, 4 * B])
        short_flag = sb("short_flag", [1, 1], I32)
        x_sb = sb("x_sb", [P, B * T, D])
        ctx_sb = sb("ctx_sb", [P, B * KT, E])
        ctxT = sb("ctxT", [P, B, M])
        wmem_sb = sb("wmem_sb", [P, K, E])
        wgate_sb = sb("wgate_sb", [P, K, 2 * D])
        gate_xT = sb("gate_xT", [P, K, D])
        gate_cT = sb("gate_cT", [P, K, D])
        gate_mem = sb("gate_mem", [P, 2 * D])
        bgate_row = sb("bgate_row", [1, D])
        normw_sb = sb("normw_sb", [P, D])
        lncol = sb("lncol", [P, 4, K])
        gates = sb("gates", [P, 4])
        q_scale = sb("q_scale", [P, K])
        q_bias = sb("q_bias", [P, PAIRS])
        h_bias = sb("h_bias", [P, FM])
        half_pow = sb("half_pow", [P, T])
        stage = sb("stage", [P, 2048])
        w1_sb = sb("w1_sb", [P, K, FF])
        wkv_sb = sb("wkv_sb", [P, 2 * INNER])
        wq_pair = sb("wq_pair", [P, 2, 2048], F32R)
        wo_pair = sb("wo_pair", [P, 2, 2048], F32R)
        th = sb("th", [P, T, D])
        fused = sb("fused", [P, T, D])
        xhat = sb("xhat", [P, T, D])
        xhT_pair = sb("xhT_pair", [P, 2, K, N], F32R)
        stats = sb("stats", [P, T, 6])
        mean_var = sb("mean_var", [P, T, 2])
        mean_var2 = sb("mean_var2", [P, B * T, 2])
        sumsq = sb("sumsq", [P, T])
        ms = sb("ms", [P, T])
        rms_r = sb("rms_r", [P, T])
        ve = sb("ve", [P, T])
        rstd = sb("rstd", [P, T])
        ve2 = sb("ve2", [P, B, T])
        rstd2 = sb("rstd2", [P, B, T])
        q_sb = sb("q_sb", [P, PAIRS, N])
        RING = 4
        neg_max = sb("neg_max", [P, RING, 4])
        row_sum = sb("row_sum", [P, RING, 4])
        row_rcp = sb("row_rcp", [P, RING, 4])
        expd = sb("expd", [P, RING, BANK])
        probs = sb("probs", [P, RING, BANK])
        probsT = sb("probsT", [P, 2, 4, N])
        oT_pair = sb("oT_pair", [P, 2, 2, 2, N], F32R)

        l0_start = nc.sbuf_base
        l0_region = sb("l0_region", [P, 2048])
        xT = l0_region[:, 0:512].rearrange("p (k n) -> p k n", k=K)
        ctx_probsT = l0_region[:, 512:1536].rearrange("p (k n) -> p k n", k=KT)
        yT = l0_region[:, 1536:1792]
        uT = l0_region[:, 1792:2048]
        kv_start = nc.sbuf_base
        k_split = sb("k_split", [P, PAIRS, KT, 2, P])
        v_sb = sb("v_sb", [P, KT, INNER])
        w2_pair = nc.alloc_sbuf_tensor_at("w2_pair", [P, 2, FM, D], F32R, offset=kv_start)
        gelu_pair = nc.alloc_sbuf_tensor_at("gelu_pair", [P, FM, 2, 2 * N], F32R, offset=kv_start + 16384)
        h2T_pair = nc.alloc_sbuf_tensor_at("h2T_pair", [P, 2, K, 2 * N], F32R, offset=l0_start)

        bank = [psum(f"bank{i}", [P, BANK]) for i in range(8)]
        GEN, PROJ, SC, SPREAD, CONTEXT = bank[0:2], bank[2], bank[3:5], bank[5:7], bank[7]

        wq_raw = stage[:, :].rearrange("p (k n) -> p k n", k=K)
        wq_p = wq_pair[:, :, :].rearrange("p h (k n) -> p h k n", k=K)
        w1_p = wq_p
        wo_p = wo_pair[:, :, :].rearrange("p h (i n) -> p h i n", n=D)

        x_in = [sem(f"x_in{b}") for b in range(B)]
        ctx_in_sem = [sem(f"ctx_in{b}") for b in range(B)]
        w_in = {n: sem(f"{n}_in") for n in ("mask", "wmem", "wgate", "bgate", "normw", "lncol", "gates", "wkv",
                                            "wq", "wo", "w1", "w2")}
        const_ready = sem("const_ready")
        flag_ready = sem("flag_ready")
        flag_step = sem("flag_step")
        pool_step = sem("pool_step")
        gates_ready = sem("gates_ready")
        out_done = sem("out_done")
        pe = {k: sem(f"pe_{k}") for k in ("xT", "ctxT", "gatew", "gatem", "qbias", "hbias", "y", "scores", "spread",
                                          "u", "gate", "xhT", "k", "v", "q", "av", "wo", "h2T", "ff1", "ff2")}
        act = {k: sem(f"act_{k}") for k in ("xT", "y", "exp", "spread", "u", "tanh", "square", "xhT", "k", "v", "o",
                                            "h2T", "gelu", "geluhi", "wsplit", "gatew")}
        dve = {k: sem(f"dve_{k}") for k in ("ctxT", "gatew", "gatem", "qbias", "hbias", "negmax", "rcp", "spread",
                                            "gated", "ms", "ve", "xhat", "xhT", "k", "v", "q", "o", "wo",
                                            "ve2", "x2hat", "h2T", "gelu", "out", "wsplit", "mask", "qscale")}
        pool = {k: sem(f"pool_{k}") for k in ("rms", "rstd", "probs", "rstd2", "wsplit")}

        PRO = list(prologue())
        plans = {nt: PRO + list(body(nt)) for nt in (1, KT)}

        def counts(nt):
            seen, place = {}, {}
            for st in plans[nt]:
                seen[st[0]] = seen.get(st[0], 0) + 1
                place[st] = seen[st[0]]
            return place

        class Path:

            def __init__(self, nt):
                self.nt = nt
                self.plan = plans[nt]
                self.at = counts(nt)
                self.units = 4 * nt
                self.heads = 4 // nt
                self.general = []
                for st in self.plan:
                    n = {"xT": 1, "ctxT": 1, "weights": 4, "qbias": 1, "y": 1, "u": 1, "gate": 2, "xhT": 1, "k": 1,
                         "v": 1, "q": 1, "hbias": 1, "h2T": 1, "ff1": 1, "ff2": 1}.get(st[0], 0)
                    self.general += [(st, i) for i in range(n)]
                self.use = {key: n for n, key in enumerate(self.general)}
                self.all_scores = T * sum(st[0] == "scores" for st in self.plan)
                assert self.all_scores % RING == 0

            def bank(self, st, i=0):
                return GEN[self.use[(st, i)] % len(GEN)]

            def bank_free(self, st, i=0):
                n = self.use[(st, i)] - len(GEN)
                if n < 0:
                    return []
                old, j = self.general[n]
                c = self.at[old]
                return {
                    "xT": [(act["xT"], c)], "ctxT": [(dve["ctxT"], c)],
                    "weights": [[(dve["gatew"], 1)], [(dve["gatew"], 2)], [(act["gatew"], 1)],
                                [(dve["gatem"], 1)]][j] if old[0] == "weights" else None,
                    "qbias": [(dve["qbias"], 1)], "hbias": [(dve["hbias"], 1)],
                    "y": [(act["y"], c)], "u": [(act["u"], c)], "gate": [(dve["gated"], T * (c - 1) + j + 1)],
                    "xhT": [(dve["xhT"], c)], "k": [(dve["k"], c), (act["k"], c)],
                    "v": [(act["v"], (c + 1) // 2)] if c % 2 else [(dve["v"], c // 2)],
                    "q": [(dve["q"], c)], "h2T": [(dve["h2T"], c)],
                    "ff1": [(act["gelu"], c)], "ff2": [(dve["out"], c)],
                }[old[0]]

            def score_no(self, kind, b, u, t):
                return T * (self.at[("scores", kind, b, u)] - 1) + t

            def last_unit(self, pair):
                return (2 * pair + 1) // self.heads

            def quads(self, b, u):
                return 4 * b + (u + 1) // self.nt

            def keys_of(self, b):
                return "hot" if self.nt == 1 else b

        paths = {nt: Path(nt) for nt in (1, KT)}

        def split_matmul(bank_ap, lhs, rhs, start, stop):
            for n, (a, c) in enumerate(((HI, HI), (HI, LO), (LO, HI))):
                last = nc.tensor.matmul(bank_ap, lhs(a), rhs(c), start=start and n == 0, stop=stop and n == 2)
            return last

        def spread_to(eng, path, st, t):
            kind, b, u = st[1:]
            if kind == "ctx":
                if b:
                    eng.wait_ge(pe["u"], b)
                return ctx_probsT[:, :, t * P:(t + 1) * P]
            unit = b * path.units + u
            if unit >= 2:
                eng.wait_ge(pe["av"], unit - 1)
            return probsT[:, unit % 2, :, t * P:(t + 1) * P]

        block = stack.enter_context(nc.Block())

        @block.sync
        def _(sp):
            def load(dst, src, s):
                sp.dma_start(dst, src).then_inc(s, 16)

            def load_x(b):
                load(x_sb[:, b * T:(b + 1) * T, :], x[b].rearrange("(t p) d -> p t d", p=P), x_in[b])

            def load_ctx(b):
                load(ctx_sb[:, b * KT:(b + 1) * KT, :], ctx_in[b].rearrange("(t p) e -> p t e", p=P), ctx_in_sem[b])

            load_x(0)
            load(wmem_sb[:, :, :], w_mem.rearrange("(p k) e -> p k e", k=K), w_in["wmem"])
            load_ctx(0)
            load(wgate_sb[:, :, :], w_gate.rearrange("(k p) f -> p k f", p=P), w_in["wgate"])
            load(bgate_row[:, :], b_gate.rearrange("(a d) -> a d", a=1), w_in["bgate"])
            for b in range(1, B):
                load_ctx(b)
            load(wkv_sb[:, :], wkv, w_in["wkv"])
            load(mask_u8[:, :], mask.rearrange("(a b) m -> a (b m)", a=1), w_in["mask"])
            load(stage[:, :].rearrange("p (k n) -> p k n", k=K), wq.rearrange("(p k) n -> p k n", k=K), w_in["wq"])
            for b in range(1, B):
                load_x(b)
            load(w1_sb[:, :, :], w1.rearrange("(p k) n -> p k n", k=K), w_in["w1"])
            sp.wait_ge(act["wsplit"], 1)
            sp.wait_ge(dve["wsplit"], 1)
            sp.wait_ge(pe["qbias"], 1)
            load(stage[:, :].rearrange("p (i n) -> p i n", n=D), wo.rearrange("(i p) n -> p i n", p=P), w_in["wo"])
            sp.wait_ge(act["wsplit"], 2)
            sp.wait_ge(pool["wsplit"], 1)
            load(stage[:, :].rearrange("p (i n) -> p i n", n=D), w2.rearrange("(i p) n -> p i n", p=P), w_in["w2"])
            for b in range(B):
                for t in range(T):
                    sp.wait_ge(dve["out"], b * T + t + 1)
                    sp.dma_start(out[b, t * P:(t + 1) * P, :], x_sb[:, b * T + t, :]).then_inc(out_done, 16)
            sp.wait_ge(out_done, 16 * B * T)

        @block.gpsimd
        def _(gp):
            nc.gpsimd.memset(ident[:, :], 0.0).then_inc(pool_step, 1)
            nc.gpsimd.memset(ones_row[:, :], 1.0).then_inc(const_ready, 1)
            nc.gpsimd.memset(ones_bf[:, :], 1.0).then_inc(const_ready, 1)
            gp.wait_ge(pool_step, 1)
            nc.gpsimd.affine_select(out=ident[:, :], in_=ident[:, :], compare_op=ALU.not_equal, fill=1.0, base=0,
                                    pattern=[[-1, P]], channel_multiplier=1).then_inc(const_ready, 1)
            nc.gpsimd.memset(half_pow[:, :], -0.5).then_inc(const_ready, 1)
            nc.gpsimd.memset(k_split[0:DH, :, :, 1, :], 0.0).then_inc(const_ready, 1)
            gp.wait_ge(const_ready, 5)
            nc.gpsimd.memset(k_split[DH:P, :, :, 0, :], 0.0).then_inc(const_ready, 1)

            def run(path, plan):
                for st in plan:
                    c = path.at[st]
                    if st[0] == "norm":
                        for t in range(T):
                            n = path.score_no(*st[1:], t)
                            r, hb = n % RING, (path.heads if st[1] == "head" else 1)
                            gp.wait_ge(dve["rcp"], n + 1)
                            if n >= RING:
                                gp.wait_ge(pe["spread"], n - RING + 1)
                            nc.gpsimd.tensor_tensor(
                                probs[:, r, :].rearrange("p (h k) -> p h k", h=hb),
                                expd[:, r, :].rearrange("p (h k) -> p h k", h=hb),
                                row_rcp[:, r, 0:hb].rearrange("p (h k) -> p h k", k=1).to_broadcast([P, hb, BANK // hb]),
                                ALU.mult).then_inc(pool["probs"], 1)
                    elif st[0] == "rms":
                        gp.wait_ge(dve["ms"], c)
                        if c > 1:
                            gp.wait_ge(dve["ve"], c - 1)
                        nc.gpsimd.tensor_tensor(rms_r[:, :], ms[:, :], half_pow[:, :], ALU.pow).then_inc(pool["rms"], 1)
                    elif st[0] == "ln1":
                        gp.wait_ge(dve["ve"], c)
                        if c > 1:
                            gp.wait_ge(dve["xhat"], c - 1)
                        nc.gpsimd.tensor_tensor(rstd[:, :], ve[:, :], half_pow[:, :], ALU.pow).then_inc(pool["rstd"], 1)
                    elif st[0] == "ln2":
                        gp.wait_ge(dve["ve2"], c)
                        nc.gpsimd.tensor_tensor(rstd2[:, st[1], :], ve2[:, st[1], :], half_pow[:, :], ALU.pow
                                                ).then_inc(pool["rstd2"], 1)
                    elif st[0] == "splito":
                        gp.wait_ge(act["wsplit"], 2)
                        nc.gpsimd.tensor_tensor(wo_pair[:, LO, :], stage[:, :], wo_pair[:, HI, :].bitcast(F32),
                                                ALU.subtract).then_inc(pool["wsplit"], 1)

            gp.wait_ge(const_ready, 6)
            run(paths[1], PRO)
            gp.wait_ge(flag_ready, 1)
            short = gp.value_load(short_flag[0:1, 0:1], min_val=0, max_val=1)
            with gp.If(short == 1):
                run(paths[1], paths[1].plan[len(PRO):])
            with gp.Else():
                run(paths[KT], paths[KT].plan[len(PRO):])

        @block.scalar
        def _(sc):
            with nc.allow_non_contiguous_dma(reason="single values"):
                sc.dma_start(gates[:, 0:1], attn_gate.rearrange("(a c) -> a c", a=1).to_broadcast([P, 1])
                             ).then_inc(w_in["gates"], 16)
                sc.dma_start(gates[:, 1:2], ff_gate.rearrange("(a c) -> a c", a=1).to_broadcast([P, 1])
                             ).then_inc(w_in["gates"], 16)
            sc.dma_start(normw_sb[:, :], norm_w.rearrange("(a d) -> a d", a=1).to_broadcast([P, D])
                         ).then_inc(w_in["normw"], 16)
            for i, v in enumerate((lnq_g, lnq_b, lnf_g, lnf_b)):
                sc.dma_start(lncol[:, i, :], v.rearrange("(p k) -> p k", k=K)).then_inc(w_in["lncol"], 16)

            def run(path, plan):
                for st in plan:
                    kind, c = st[0], path.at[st]
                    if kind == "xT":
                        b = st[1]
                        sc.wait_ge(pe["xT"], c)
                        if b:
                            sc.wait_ge(pe["gate"], T * b)
                        nc.scalar.copy(xT, path.bank(st)[:, :].rearrange("p (k n) -> p k n", k=K)
                                       ).then_inc(act["xT"], 1)
                    elif kind == "weights":
                        sc.wait_ge(pe["gatew"], 3)
                        nc.scalar.copy(gate_mem[:, D:2 * D].rearrange("e (p k) -> e k p", k=K),
                                       path.bank(st, 2)[:, 0:D].rearrange("e (k p) -> e k p", k=K)
                                       ).then_inc(act["gatew"], 1)
                    elif kind == "mask":
                        sc.wait_ge(w_in["gates"], 32)
                        nc.scalar.activation(gates[:, 2:4], gates[:, 0:2], ACT.Tanh).then_inc(gates_ready, 1)
                    elif kind == "y":
                        sc.wait_ge(pe["y"], c)
                        if c > 1:
                            sc.wait_ge(pe["scores"], path.score_no("ctx", st[1] - 1, 0, T - 1) + 1)
                        nc.scalar.activation(yT, path.bank(st)[:, 0:N], ACT.Copy, scale=D ** -0.5
                                             ).then_inc(act["y"], 1)
                    elif kind == "exp":
                        for t in range(T):
                            n = path.score_no(*st[1:], t)
                            r, hb = n % RING, (path.heads if st[1] == "head" else 1)
                            sc.wait_ge(dve["negmax"], n + 1)
                            if n >= RING:
                                sc.wait_ge(pool["probs"], n - RING + 1)
                            w = BANK // hb
                            for h in range(hb):
                                last = nc.scalar.activation(
                                    expd[:, r, h * w:(h + 1) * w], SC[n % 2][:, h * w:(h + 1) * w], ACT.Exp,
                                    bias=neg_max[:, r, h:h + 1], accum_out=row_sum[:, r, h:h + 1])
                            last.then_inc(act["exp"], 1)
                    elif kind == "spread":
                        n = path.score_no(*st[1:], 0)
                        sc.wait_ge(pe["spread"], n + 1)
                        nc.scalar.copy(spread_to(sc, path, st, 0),
                                       SPREAD[n % 2][:, :].rearrange("p (j n) -> p j n", j=4)
                                       ).then_inc(act["spread"], 1)
                    elif kind == "u":
                        sc.wait_ge(pe["u"], c)
                        if c > 1:
                            sc.wait_ge(pe["gate"], T * (c - 1))
                        nc.scalar.copy(uT, path.bank(st)[:, 0:N]).then_inc(act["u"], 1)
                    elif kind == "gate":
                        for t in range(T):
                            sc.wait_ge(pe["gate"], T * (c - 1) + t + 1)
                            if c > 1:
                                sc.wait_ge(act["square"], c - 1)
                            nc.scalar.activation(th[:, t, :], path.bank(st, t)[:, 0:D], ACT.Tanh, scale=0.5
                                                 ).then_inc(act["tanh"], 1)
                    elif kind == "fuse":
                        for t in range(T):
                            sc.wait_ge(dve["gated"], T * (c - 1) + t + 1)
                            last = nc.scalar.activation(th[:, t, :], fused[:, t, :], ACT.Square,
                                                        accum_out=sumsq[:, t:t + 1])
                        last.then_inc(act["square"], 1)
                    elif kind == "xhT":
                        sc.wait_ge(pe["xhT"], c)
                        if c > 1:
                            sc.wait_ge(pe["q"], path.at[("q", st[1] - 1, 3)])
                        nc.scalar.copy(xhT_pair[:, HI, :, :], path.bank(st)[:, :].rearrange("p (k n) -> p k n", k=K)
                                       ).then_inc(act["xhT"], 1)
                    elif kind == "k":
                        sc.wait_ge(pe["k"], c)
                        if c > PAIRS:
                            sc.wait_ge(act["k"], c - PAIRS)
                        nc.scalar.copy(k_split[0:DH, st[2], :, 0, :],
                                       path.bank(st)[0:DH, :].rearrange("p (s n) -> p s n", s=KT)
                                       ).then_inc(act["k"], 1)
                    elif kind == "v" and st[3] == 0:
                        sc.wait_ge(pe["v"], c)
                        if c > 2 * KT:
                            sc.wait_ge(act["v"], (c + 1) // 2 - KT)
                        nc.scalar.copy(v_sb[:, st[2], 0:BANK], path.bank(st)[:, :]).then_inc(act["v"], 1)
                    elif kind == "av":
                        b, u = st[1:]
                        if (u + 1) % path.nt == 0:
                            g = path.quads(b, u)
                            sc.wait_ge(pe["av"], c)
                            if g > 2:
                                sc.wait_ge(pe["wo"], g - 2)
                            nc.scalar.copy(oT_pair[:, HI, (g - 1) % 2, :, :],
                                           CONTEXT[:, :].rearrange("p (j n) -> p j n", j=2)).then_inc(act["o"], 1)
                    elif kind == "splitq":
                        sc.wait_ge(w_in["wq"], 16)
                        sc.wait_ge(dve["qscale"], 1)
                        for k in range(K):
                            last = nc.scalar.activation(wq_p[:, HI, k, :], wq_raw[:, k, :], ACT.Copy,
                                                        scale=q_scale[:, k:k + 1])
                        last.then_inc(act["wsplit"], 1)
                    elif kind == "splito":
                        sc.wait_ge(w_in["wo"], 16)
                        nc.scalar.copy(wo_pair[:, HI, :], stage[:, :]).then_inc(act["wsplit"], 1)
                    elif kind == "split1":
                        sc.wait_ge(w_in["w1"], 16)
                        sc.wait_ge(pe["q"], path.at[("q", B - 1, 3)])
                        for k in range(K):
                            last = nc.scalar.activation(w1_p[:, HI, k, :], w1_sb[:, k, :], ACT.Copy,
                                                        scale=lncol[:, 2, k:k + 1])
                        last.then_inc(act["wsplit"], 1)
                    elif kind == "split2":
                        sc.wait_ge(w_in["w2"], 16)
                        sc.wait_ge(pe["scores"], path.score_no("head", B - 1, path.units - 1, T - 1) + 1)
                        nc.scalar.copy(w2_pair[:, HI, :, :], stage[:, :].rearrange("p (i n) -> p i n", n=D)
                                       ).then_inc(act["wsplit"], 1)
                    elif kind == "h2T":
                        f, half = st[1:]
                        sc.wait_ge(pe["h2T"], c)
                        if f:
                            sc.wait_ge(pe["ff1"], FM * f)
                        else:
                            sc.wait_ge(pe["gate"], T * B)
                        nc.scalar.copy(h2T_pair[:, HI, :, half * N:(half + 1) * N],
                                       path.bank(st)[:, :].rearrange("p (k n) -> p k n", k=K)
                                       ).then_inc(act["h2T"], 1)
                    elif kind == "ff1":
                        f, m = st[1:]
                        sc.wait_ge(pe["ff1"], c)
                        if c == 1:
                            sc.wait_ge(dve["hbias"], 1)
                        if c > RING:
                            sc.wait_ge(dve["gelu"], c - RING)
                        else:
                            sc.wait_ge(pool["probs"], path.all_scores - RING + c)
                        nc.scalar.activation(expd[:, (c - 1) % RING, :], path.bank(st)[:, :], ACT.Gelu,
                                             bias=h_bias[:, m:m + 1]).then_inc(act["gelu"], 1)
                        if f:
                            sc.wait_ge(pe["ff2"], 2 * T * f)
                        elif m == 0:
                            sc.wait_ge(pe["scores"], path.all_scores)
                        elif m == FM // 2:
                            sc.wait_ge(pe["av"], path.at[("av", B - 1, path.units - 1)])
                        sc.wait_ge(act["gelu"], c)
                        nc.scalar.copy(gelu_pair[:, m, HI, :], expd[:, (c - 1) % RING, :]).then_inc(act["geluhi"], 1)

            run(paths[1], PRO)
            sc.wait_ge(flag_ready, 1)
            short = sc.value_load(short_flag[0:1, 0:1], min_val=0, max_val=1)
            with sc.If(short == 1):
                run(paths[1], paths[1].plan[len(PRO):])
            with sc.Else():
                run(paths[KT], paths[KT].plan[len(PRO):])

        @block.vector
        def _(ve_):
            def chain(ins):
                flag_count[0] += 1
                ins.then_inc(flag_step, 1)
                ve_.wait_ge(flag_step, flag_count[0])

            flag_count = [0]

            def norm_stats(tiles, dst, b_tiles):
                for i, t in enumerate(tiles):
                    last = nc.vector.bn_stats(stats[:, i, :], x_sb[:, t, :])
                chain(last)
                for i, t in enumerate(tiles):
                    last = nc.vector.bn_aggr(dst[:, b_tiles + i, :], stats[:, i, :])
                chain(last)

            def run(path, plan):
                for st in plan:
                    kind, c = st[0], path.at[st]
                    if kind == "ctxT":
                        ve_.wait_ge(pe["ctxT"], c)
                        nc.vector.tensor_copy(ctxT[:, st[1], :], path.bank(st)[:, :]).then_inc(dve["ctxT"], 1)
                    elif kind == "weights":
                        for i, dst in enumerate((gate_xT, gate_cT)):
                            ve_.wait_ge(pe["gatew"], i + 1)
                            nc.vector.tensor_copy(dst[:, :, :], path.bank(st, i)[:, :].rearrange("p (k n) -> p k n", k=K)
                                                  ).then_inc(dve["gatew"], 1)
                        ve_.wait_ge(pe["gatem"], 1)
                        nc.vector.tensor_copy(gate_mem[:, 0:D], path.bank(st, 3)[:, 0:D]).then_inc(dve["gatem"], 1)
                    elif kind == "mask":
                        ve_.wait_ge(w_in["mask"], 16)
                        nc.vector.tensor_scalar(mask_bias[:, :], mask_u8[:, :], 1.0, -MASKED, ALU.subtract, ALU.mult
                                                ).then_inc(dve["mask"], 1)
                        chain(nc.vector.reduce_max(tile_any[:, :], mask_u8[:, :].rearrange("a (t n) -> a t n", n=P), AX_X))
                        any_v = tile_any[:, :].rearrange("a (b t) -> a b t", t=KT)
                        chain(nc.vector.reduce_max(flag_work[:, 0:B], any_v[:, :, 0:HOT], AX_X))
                        chain(nc.vector.tensor_scalar(flag_work[:, B:2 * B], flag_work[:, 0:B], -1.0, 1.0, ALU.mult, ALU.add))
                        chain(nc.vector.tensor_tensor(flag_work[:, 2 * B:3 * B], flag_work[:, B:2 * B], any_v[:, :, HOT], ALU.mult))
                        nc.vector.tensor_reduce(short_flag[:, :], flag_work[:, 2 * B:3 * B], AX_X, ALU.min).then_inc(flag_ready, 1)
                    elif kind == "qbias":
                        ve_.wait_ge(pe["qbias"], 1)
                        nc.vector.tensor_scalar(q_bias[:, :], path.bank(st)[:, 0:PAIRS], DH ** -0.5, None, ALU.mult
                                                ).then_inc(dve["qbias"], 1)
                    elif kind == "hbias":
                        ve_.wait_ge(pe["hbias"], 1)
                        nc.vector.tensor_copy(h_bias[:, :], path.bank(st)[:, 0:FM]).then_inc(dve["hbias"], 1)
                    elif kind == "scores":
                        for t in range(T):
                            n = path.score_no(*st[1:], t)
                            r, hb = n % RING, (path.heads if st[1] == "head" else 1)
                            ve_.wait_ge(pe["scores"], n + 1)
                            nc.vector.tensor_reduce(neg_max[:, r, 0:hb],
                                                    SC[n % 2][:, :].rearrange("p (h k) -> p h k", h=hb),
                                                    AX_X, ALU.max, negate=True).then_inc(dve["negmax"], 1)
                    elif kind == "norm":
                        for t in range(T):
                            n = path.score_no(*st[1:], t)
                            r, hb = n % RING, (path.heads if st[1] == "head" else 1)
                            ve_.wait_ge(act["exp"], n + 1)
                            nc.vector.reciprocal(row_rcp[:, r, 0:hb], row_sum[:, r, 0:hb]).then_inc(dve["rcp"], 1)
                    elif kind == "spread":
                        n = path.score_no(*st[1:], 1)
                        ve_.wait_ge(pe["spread"], n + 1)
                        nc.vector.tensor_copy(spread_to(ve_, path, st, 1),
                                              SPREAD[n % 2][:, :].rearrange("p (j n) -> p j n", j=4)
                                              ).then_inc(dve["spread"], 1)
                    elif kind == "gate":
                        for t in range(T):
                            ve_.wait_ge(act["tanh"], T * (c - 1) + t + 1)
                            if c > 1:
                                ve_.wait_ge(act["square"], c - 1)
                            chain(nc.vector.scalar_tensor_tensor(
                                fused[:, t, :], th[:, t, :], 1.0, path.bank(st, t)[:, D:2 * D], ALU.add, ALU.mult))
                            gated = nc.vector.scalar_tensor_tensor(
                                fused[:, t, :], fused[:, t, :], 0.5, x_sb[:, st[1] * T + t, :], ALU.mult, ALU.add)
                            gated.then_inc(dve["gated"], 1)
                    elif kind == "rms":
                        ve_.wait_ge(act["square"], c)
                        nc.vector.tensor_scalar(ms[:, :], sumsq[:, :], 1.0 / D, RMS_EPS, ALU.mult, ALU.add
                                                ).then_inc(dve["ms"], 1)
                    elif kind == "ln1":
                        b = st[1]
                        ve_.wait_ge(pool["rms"], c)
                        if c == 1:
                            ve_.wait_ge(w_in["normw"], 16)
                        for t in range(T):
                            last = nc.vector.scalar_tensor_tensor(
                                x_sb[:, b * T + t, :], fused[:, t, :], rms_r[:, t:t + 1], normw_sb[:, :],
                                ALU.mult, ALU.mult)
                        chain(last)
                        norm_stats(range(b * T, b * T + T), mean_var, 0)
                        nc.vector.tensor_scalar(ve[:, :], mean_var[:, :, 1], LN_EPS, None, ALU.add
                                                ).then_inc(dve["ve"], 1)
                    elif kind == "xhat":
                        b = st[1]
                        ve_.wait_ge(pool["rstd"], c)
                        if c > 1:
                            ve_.wait_ge(pe["xhT"], c - 1)
                        for t in range(T):
                            last = nc.vector.tensor_scalar(xhat[:, t, :], x_sb[:, b * T + t, :], mean_var[:, t, 0:1],
                                                           rstd[:, t:t + 1], ALU.subtract, ALU.mult)
                        last.then_inc(dve["xhat"], 1)
                    elif kind == "xhT":
                        ve_.wait_ge(act["xhT"], c)
                        nc.vector.tensor_tensor(xhT_pair[:, LO, :, :],
                                                path.bank(st)[:, :].rearrange("p (k n) -> p k n", k=K),
                                                xhT_pair[:, HI, :, :].bitcast(F32), ALU.subtract
                                                ).then_inc(dve["xhT"], 1)
                    elif kind == "k":
                        ve_.wait_ge(pe["k"], c)
                        if c > PAIRS:
                            ve_.wait_ge(dve["k"], c - PAIRS)
                        nc.vector.tensor_copy(k_split[DH:P, st[2], :, 1, :],
                                              path.bank(st)[DH:P, :].rearrange("p (s n) -> p s n", s=KT)
                                              ).then_inc(dve["k"], 1)
                    elif kind == "v" and st[3] == 1:
                        ve_.wait_ge(pe["v"], c)
                        if c > 2 * KT:
                            ve_.wait_ge(dve["v"], c // 2 - KT)
                        nc.vector.tensor_copy(v_sb[:, st[2], BANK:2 * BANK], path.bank(st)[:, :]).then_inc(dve["v"], 1)
                    elif kind == "q":
                        b, j = st[1:]
                        ve_.wait_ge(pe["q"], c)
                        if c == 1:
                            ve_.wait_ge(dve["qbias"], 1)
                        if b:
                            ve_.wait_ge(pe["scores"],
                                        path.score_no("head", b - 1, path.last_unit(2 * j + 1), T - 1) + 1)
                        for i in range(2):
                            pair = 2 * j + i
                            last = nc.vector.tensor_scalar(q_sb[:, pair, :], path.bank(st)[:, i * N:(i + 1) * N],
                                                           q_bias[:, pair:pair + 1], None, ALU.add)
                        last.then_inc(dve["q"], 1)
                    elif kind == "av":
                        b, u = st[1:]
                        if (u + 1) % path.nt == 0:
                            g = path.quads(b, u)
                            ve_.wait_ge(act["o"], g)
                            nc.vector.tensor_tensor(oT_pair[:, LO, (g - 1) % 2, :, :],
                                                    CONTEXT[:, :].rearrange("p (j n) -> p j n", j=2),
                                                    oT_pair[:, HI, (g - 1) % 2, :, :].bitcast(F32), ALU.subtract
                                                    ).then_inc(dve["o"], 1)
                    elif kind == "splitq":
                        ve_.wait_ge(act["wsplit"], 1)
                        for k in range(K):
                            last = nc.vector.scalar_tensor_tensor(
                                wq_p[:, LO, k, :], wq_raw[:, k, :], q_scale[:, k:k + 1],
                                wq_p[:, HI, k, :].bitcast(F32), ALU.mult, ALU.subtract)
                        last.then_inc(dve["wsplit"], 1)
                    elif kind == "split1":
                        ve_.wait_ge(act["wsplit"], 3)
                        for k in range(K):
                            last = nc.vector.scalar_tensor_tensor(
                                w1_p[:, LO, k, :], w1_sb[:, k, :], lncol[:, 2, k:k + 1],
                                w1_p[:, HI, k, :].bitcast(F32), ALU.mult, ALU.subtract)
                        last.then_inc(dve["wsplit"], 1)
                    elif kind == "split2":
                        ve_.wait_ge(act["wsplit"], 4)
                        nc.vector.tensor_tensor(w2_pair[:, LO, :, :], stage[:, :].rearrange("p (i n) -> p i n", n=D),
                                                w2_pair[:, HI, :, :].bitcast(F32), ALU.subtract
                                                ).then_inc(dve["wsplit"], 1)
                    elif kind == "wo" and st[2] == 3:
                        b = st[1]
                        ve_.wait_ge(pe["wo"], c)
                        if b == 0:
                            ve_.wait_ge(gates_ready, 1)
                        nc.vector.scalar_tensor_tensor(
                            x_sb[:, b * T:b * T + T, :], PROJ[:, :].rearrange("p (t n) -> p t n", t=T),
                            gates[:, 2:3], x_sb[:, b * T:b * T + T, :], ALU.mult, ALU.add).then_inc(dve["wo"], 1)
                    elif kind == "ln2":
                        b = st[1]
                        ve_.wait_ge(dve["wo"], b + 1)
                        norm_stats(range(b * T, b * T + T), mean_var2, b * T)
                        nc.vector.tensor_scalar(ve2[:, b, :], mean_var2[:, b * T:b * T + T, 1], LN_EPS, None, ALU.add
                                                ).then_inc(dve["ve2"], 1)
                    elif kind == "x2hat":
                        b = st[1]
                        ve_.wait_ge(pool["rstd2"], path.at[("ln2", b)])
                        if c == 1:
                            ve_.wait_ge(pe["xhT"], B)
                        else:
                            ve_.wait_ge(pe["h2T"], c - 1)
                        for t in range(T):
                            last = nc.vector.tensor_scalar(xhat[:, t, :], x_sb[:, b * T + t, :],
                                                           mean_var2[:, b * T + t, 0:1], rstd2[:, b, t:t + 1],
                                                           ALU.subtract, ALU.mult)
                        last.then_inc(dve["x2hat"], 1)
                    elif kind == "h2T":
                        f, half = st[1:]
                        ve_.wait_ge(act["h2T"], c)
                        nc.vector.tensor_tensor(h2T_pair[:, LO, :, half * N:(half + 1) * N],
                                                path.bank(st)[:, :].rearrange("p (k n) -> p k n", k=K),
                                                h2T_pair[:, HI, :, half * N:(half + 1) * N].bitcast(F32),
                                                ALU.subtract).then_inc(dve["h2T"], 1)
                    elif kind == "ff1":
                        f, m = st[1:]
                        ve_.wait_ge(act["geluhi"], c)
                        nc.vector.tensor_tensor(gelu_pair[:, m, LO, :], expd[:, (c - 1) % RING, :],
                                                gelu_pair[:, m, HI, :].bitcast(F32), ALU.subtract
                                                ).then_inc(dve["gelu"], 1)
                    elif kind == "ff2":
                        f, i = st[1:]
                        tile = 2 * T * f + i
                        ve_.wait_ge(pe["ff2"], c)
                        nc.vector.scalar_tensor_tensor(
                            x_sb[:, tile, :], path.bank(st)[:, 0:D], gates[:, 3:4], x_sb[:, tile, :],
                            ALU.mult, ALU.add).then_inc(dve["out"], 1)

            ve_.wait_ge(w_in["lncol"], 64)
            nc.vector.tensor_scalar(q_scale[:, :], lncol[:, 0, :], DH ** -0.5, None, ALU.mult).then_inc(dve["qscale"], 1)
            ve_.wait_ge(dve["qscale"], 1)
            run(paths[1], PRO)
            before = flag_count[0]
            ve_.wait_ge(flag_ready, 1)
            short = ve_.value_load(short_flag[0:1, 0:1], min_val=0, max_val=1)
            with ve_.If(short == 1):
                run(paths[1], paths[1].plan[len(PRO):])
            with ve_.Else():
                flag_count[0] = before
                run(paths[KT], paths[KT].plan[len(PRO):])

        @block.tensor
        def _(te):
            def free(path, st, i=0):
                for s, v in path.bank_free(st, i):
                    te.wait_ge(s, v)

            def run(path, plan):
                for st in plan:
                    kind, c = st[0], path.at[st]
                    if kind == "xT":
                        b = st[1]
                        te.wait_ge(x_in[b], 16)
                        free(path, st)
                        for k in range(K):
                            for t in range(T):
                                last = nc.tensor.transpose(path.bank(st)[:, k * N + t * P:k * N + (t + 1) * P],
                                                           x_sb[:, b * T + t, k:D:K], ident[:, :])
                        last.then_inc(pe["xT"], 1)
                    elif kind == "ctxT":
                        b = st[1]
                        te.wait_ge(ctx_in_sem[b], 16)
                        free(path, st)
                        for j in range(KT):
                            last = nc.tensor.transpose(path.bank(st)[:, j * P:(j + 1) * P], ctx_sb[:, b * KT + j, :],
                                                       ident[:, :])
                        last.then_inc(pe["ctxT"], 1)
                    elif kind == "weights":
                        te.wait_ge(w_in["wgate"], 16)
                        for i in range(2):
                            free(path, st, i)
                            for k in range(K):
                                for dt in range(K):
                                    last = nc.tensor.transpose(
                                        path.bank(st, i)[:, k * D + dt * P:k * D + (dt + 1) * P],
                                        wgate_sb[:, dt, i * D + k:(i + 1) * D:K], ident[:, :])
                            last.then_inc(pe["gatew"], 1)
                        free(path, st, 2)
                        for k in range(K):
                            last = nc.tensor.transpose(path.bank(st, 2)[:, k * P:(k + 1) * P], wmem_sb[:, k, :],
                                                       ident[:, :])
                        last.then_inc(pe["gatew"], 1)
                        te.wait_ge(dve["gatew"], 2)
                        free(path, st, 3)
                        for k in range(K):
                            last = nc.tensor.matmul(path.bank(st, 3)[:, 0:D], wmem_sb[:, k, :], gate_cT[:, k, :],
                                                    start=k == 0, stop=k == K - 1)
                        last.then_inc(pe["gatem"], 1)
                    elif kind in ("qbias", "hbias"):
                        if kind == "qbias":
                            te.wait_ge(w_in["wq"], 16)
                            te.wait_ge(w_in["lncol"], 64)
                        else:
                            te.wait_ge(w_in["w1"], 16)
                        free(path, st)
                        shift = lncol[:, 1 if kind == "qbias" else 3, :]
                        weights = wq_raw if kind == "qbias" else w1_sb
                        for m in range(PAIRS):
                            for k in range(K):
                                last = nc.tensor.matmul(path.bank(st)[:, m:m + 1], weights[:, k, m * P:(m + 1) * P],
                                                        shift[:, k:k + 1], start=k == 0, stop=k == K - 1)
                        last.then_inc(pe[kind], 1)
                    elif kind == "y":
                        if c == 1:
                            te.wait_ge(w_in["wmem"], 16)
                        te.wait_ge(act["xT"], c)
                        free(path, st)
                        for k in range(K):
                            last = nc.tensor.matmul(path.bank(st)[:, 0:N], wmem_sb[:, k, :], xT[:, k, :],
                                                    start=k == 0, stop=k == K - 1)
                        last.then_inc(pe["y"], 1)
                    elif kind == "scores":
                        what, b, u = st[1:]
                        for t in range(T):
                            n = path.score_no(what, b, u, t)
                            if n >= 2:
                                te.wait_ge(act["exp"], n - 1)
                            toks = slice(t * P, (t + 1) * P)
                            if what == "ctx":
                                if t == 0:
                                    te.wait_ge(act["y"], path.at[("y", b)])
                                    te.wait_ge(dve["ctxT"], path.at[("ctxT", b)])
                                last = nc.tensor.matmul(SC[n % 2][:, :], yT[:, toks], ctxT[:, b, :],
                                                        start=True, stop=True)
                            else:
                                if t == 0:
                                    te.wait_ge(dve["q"], path.at[("q", b, (u * path.heads) // 4)])
                                    if u == 0:
                                        keys = path.at[("k", path.keys_of(b), PAIRS - 1)]
                                        te.wait_ge(act["k"], keys)
                                        te.wait_ge(dve["k"], keys)
                                        te.wait_ge(const_ready, 6)
                                if path.nt == 1:
                                    kept = mask_bias[0:1, b * M + HOT * P:b * M + (HOT + 1) * P]
                                    bias = kept.rearrange("a (h k) -> a h k", h=1).to_broadcast([1, 4, P])
                                    nc.tensor.matmul(SC[n % 2][:, :].rearrange("p (h k) -> p h k", h=4),
                                                     ones_bf[0:1, :], bias, start=True, stop=False)
                                    for i in range(2):
                                        last = nc.tensor.matmul(
                                            SC[n % 2][:, i * 2 * P:(i + 1) * 2 * P], q_sb[:, 2 * u + i, toks],
                                            k_split[:, 2 * u + i, b, :, :], start=False, stop=i == 1)
                                else:
                                    nc.tensor.matmul(SC[n % 2][:, :], ones_bf[0:1, :],
                                                     mask_bias[0:1, b * M:(b + 1) * M], start=True, stop=False)
                                    last = nc.tensor.matmul(
                                        SC[n % 2][:, :].rearrange("p (s k) -> p s k", s=KT), q_sb[:, u // 2, toks],
                                        k_split[:, u // 2, :, u % 2, :], start=False, stop=True)
                            last.then_inc(pe["scores"], 1)
                    elif kind == "spread":
                        for t in range(T):
                            n = path.score_no(*st[1:], t)
                            te.wait_ge(pool["probs"], n + 1)
                            if n >= 2:
                                te.wait_ge((act, dve)[t]["spread"], n // 2)
                            for j in range(4):
                                last = nc.tensor.transpose(SPREAD[n % 2][:, j * P:(j + 1) * P],
                                                           probs[:, n % RING, j * P:(j + 1) * P], ident[:, :])
                            last.then_inc(pe["spread"], 1)
                    elif kind == "u":
                        b = st[1]
                        m = path.at[("spread", "ctx", b, 0)]
                        te.wait_ge(act["spread"], m)
                        te.wait_ge(dve["spread"], m)
                        free(path, st)
                        for j in range(KT):
                            last = nc.tensor.matmul(path.bank(st)[:, 0:N], ctx_sb[:, b * KT + j, :],
                                                    ctx_probsT[:, j, :], start=j == 0, stop=j == KT - 1)
                        last.then_inc(pe["u"], 1)
                    elif kind == "gate":
                        te.wait_ge(act["u"], c)
                        if c == 1:
                            te.wait_ge(dve["gatem"], 1)
                            te.wait_ge(act["gatew"], 1)
                            te.wait_ge(w_in["bgate"], 16)
                        for t in range(T):
                            toks = slice(t * P, (t + 1) * P)
                            free(path, st, t)
                            out_b = path.bank(st, t)
                            nc.tensor.matmul(out_b[:, :], uT[:, toks], gate_mem[:, :], start=True, stop=False)
                            nc.tensor.matmul(out_b[:, 0:D], ones_row[0:1, :], bgate_row[0:1, :], start=False,
                                             stop=False)
                            for k in range(K):
                                last = nc.tensor.matmul(out_b[:, 0:D], xT[:, k, toks], gate_xT[:, k, :],
                                                        start=False, stop=k == K - 1)
                            last.then_inc(pe["gate"], 1)
                    elif kind in ("xhT", "h2T"):
                        te.wait_ge(dve["xhat" if kind == "xhT" else "x2hat"], c)
                        free(path, st)
                        for k in range(K):
                            for t in range(T):
                                last = nc.tensor.transpose(path.bank(st)[:, k * N + t * P:k * N + (t + 1) * P],
                                                           xhat[:, t, k:D:K], ident[:, :])
                        last.then_inc(pe[kind], 1)
                    elif kind == "k":
                        b, pair = st[1:]
                        if c == 1:
                            te.wait_ge(w_in["wkv"], 16)
                            te.wait_ge(dve["ctxT"], B)
                        free(path, st)
                        keys = ctxT[:, :, HOT * P:M] if b == "hot" else ctxT[:, b, :]
                        nc.tensor.matmul(
                            path.bank(st)[:, :].rearrange("p (s n) -> p s n", s=KT) if b == "hot"
                            else path.bank(st)[:, :],
                            wkv_sb[:, pair * P:(pair + 1) * P], keys, start=True, stop=True).then_inc(pe["k"], 1)
                    elif kind == "v":
                        b, s, h = st[1:]
                        free(path, st)
                        keys = ctxT[:, s, HOT * P:M] if b == "hot" else ctxT[:, b, s * P:(s + 1) * P]
                        nc.tensor.matmul(path.bank(st)[:, :], keys,
                                         wkv_sb[:, INNER + h * BANK:INNER + (h + 1) * BANK],
                                         start=True, stop=True).then_inc(pe["v"], 1)
                    elif kind == "q":
                        b, j = st[1:]
                        if j == 0:
                            te.wait_ge(dve["xhT"], path.at[("xhT", b)])
                            if b == 0:
                                te.wait_ge(dve["wsplit"], 1)
                        free(path, st)
                        for i in range(2):
                            pair = slice((2 * j + i) * P, (2 * j + i + 1) * P)
                            for k in range(K):
                                last = split_matmul(path.bank(st)[:, i * N:(i + 1) * N],
                                                    lambda a: wq_p[:, a, k, pair], lambda a: xhT_pair[:, a, k, :],
                                                    k == 0, k == K - 1)
                        last.then_inc(pe["q"], 1)
                    elif kind == "av":
                        b, u = st[1:]
                        m = path.at[("spread", "head", b, u)]
                        unit = b * path.units + u
                        te.wait_ge(act["spread"], m)
                        te.wait_ge(dve["spread"], m)
                        if u == 0:
                            values = path.at[("v", path.keys_of(b), KT - 1, 1)] // 2
                            te.wait_ge(act["v"], values)
                            te.wait_ge(dve["v"], values)
                        if u % path.nt == 0:
                            done = path.quads(b, u) - (1 if path.nt == 1 else 0)
                            if done:
                                te.wait_ge(dve["o"], done)
                        if path.nt == 1:
                            for h in range(4):
                                head, half = 4 * u + h, h % 2
                                last = nc.tensor.matmul(
                                    CONTEXT[half * DH:(half + 1) * DH, (h // 2) * N:(h // 2 + 1) * N],
                                    v_sb[:, b, head * DH:(head + 1) * DH], probsT[:, unit % 2, h, :],
                                    start=True, stop=True)
                        else:
                            half, col = u % 2, (u % 4) // 2
                            for s in range(KT):
                                last = nc.tensor.matmul(
                                    CONTEXT[half * DH:(half + 1) * DH, col * N:(col + 1) * N],
                                    v_sb[:, s, u * DH:(u + 1) * DH], probsT[:, unit % 2, s, :],
                                    start=s == 0, stop=s == KT - 1)
                        last.then_inc(pe["av"], 1)
                    elif kind == "wo":
                        b, g = st[1:]
                        te.wait_ge(dve["o"], c)
                        if b == 0 and g == 0:
                            te.wait_ge(pool["wsplit"], 1)
                        if b and g == 0:
                            te.wait_ge(dve["wo"], b)
                        for t in range(T):
                            toks = slice(t * P, (t + 1) * P)
                            for i in range(2):
                                last = split_matmul(PROJ[:, t * D:(t + 1) * D],
                                                    lambda a: oT_pair[:, a, (c - 1) % 2, i, toks],
                                                    lambda a: wo_p[:, a, 2 * g + i, :],
                                                    g == 0 and t == 0 and i == 0, g == 3 and t == T - 1 and i == 1)
                        last.then_inc(pe["wo"], 1)
                    elif kind == "ff1":
                        f, m = st[1:]
                        if m == 0:
                            te.wait_ge(dve["h2T"], 2 * (f + 1))
                            if f == 0:
                                te.wait_ge(dve["wsplit"], 2)
                        free(path, st)
                        for k in range(K):
                            last = split_matmul(path.bank(st)[:, :], lambda a: w1_p[:, a, k, m * P:(m + 1) * P],
                                                lambda a: h2T_pair[:, a, k, :], k == 0, k == K - 1)
                        last.then_inc(pe["ff1"], 1)
                    elif kind == "ff2":
                        f, i = st[1:]
                        toks = slice(i * P, (i + 1) * P)
                        if i == 0 and f == 0:
                            te.wait_ge(dve["wsplit"], 3)
                        free(path, st)
                        for m in range(FM):
                            if i == 0:
                                te.wait_ge(dve["gelu"], FM * f + m + 1)
                            last = split_matmul(path.bank(st)[:, 0:D], lambda a: gelu_pair[:, m, a, toks],
                                                lambda a: w2_pair[:, a, m, :], m == 0, m == FM - 1)
                        last.then_inc(pe["ff2"], 1)

            te.wait_ge(const_ready, 3)
            run(paths[1], PRO)
            te.wait_ge(flag_ready, 1)
            te.wait_ge(dve["mask"], 1)
            short = te.value_load(short_flag[0:1, 0:1], min_val=0, max_val=1)
            with te.If(short == 1):
                run(paths[1], paths[1].plan[len(PRO):])
            with te.Else():
                run(paths[KT], paths[KT].plan[len(PRO):])


_INS = ['x', 'ctx_1024', 'mask_BxS2_bk0', 'L0_xattn_W_mem', 'L0_xattn_W_gate', 'L0_xattn_b_gate', 'L0_xattn_norm_w',
        'L1_xattn_ln_q_g', 'L1_xattn_ln_q_b', 'L1_xattn_Wq', 'L1_xattn_Wkv', 'L1_xattn_Wo', 'L1_xattn_attn_gate',
        'L1_xattn_ln_ff_g', 'L1_xattn_ln_ff_b', 'L1_xattn_W1', 'L1_xattn_W2', 'L1_xattn_ff_gate']


def kernel(**inputs):
    import numpy as _np
    import concourse.bacc as _bacc
    from concourse import mybir as _mybir
    from concourse.bass_utils import run_bass_kernel_spmd as _run

    nc = _bacc.Bacc("TRN2", target_bir_lowering=False, num_devices=1)
    arrays, args = {}, []
    for name in _INS:
        a = _np.ascontiguousarray(inputs[name])
        arrays[f"in_{name}_dram"] = a
        args.append(nc.dram_tensor(f"in_{name}_dram", a.shape, _mybir.dt.from_np(a.dtype), kind="ExternalInput").ap())
    shape = inputs['x'].shape
    args.append(nc.dram_tensor("out_0_dram", shape, _mybir.dt.float32, kind="ExternalOutput").ap())
    gated_attention_block(nc, *args)
    r = _run(nc, [arrays], core_ids=[0])
    return r.results[0]["out_0_dram"]
```

```python
from contextlib import ExitStack

import concourse.bass as bass
from concourse import mybir

F32 = mybir.dt.float32
F32R = mybir.dt.float32r
BF16 = mybir.dt.bfloat16
U8 = mybir.dt.uint8
I32 = mybir.dt.int32
ALU = mybir.AluOpType
ACT = mybir.ActivationFunctionType
AX_X = mybir.AxisListType.X

P = 128
BANK = 512
HI, LO = 0, 1
MASKED = -(2.0 ** 100)
RMS_EPS = 1e-6
LN_EPS = 1e-5
WARM_UP = 8

PROLOGUE = (
    ("wmem",), ("xT", 0), ("ctxT", 0), ("y", 0), ("scores", "ctx", 0, 0), ("exp", "ctx", 0, 0), ("ctxT", 2),
    ("ctxT", 1), ("norm", "ctx", 0, 0), ("weights",), ("spread", "ctx", 0, 0), ("mask",), ("ctxT", 3), ("u", 0),
    ("k", "hot", 0), ("splitq", 0), ("k", "hot", 3), ("gate", 0), ("k", "hot", 1), ("fuse", 0), ("rms", 0),
    ("k", "hot", 2), ("k", "hot", 4), ("xT", 1), ("x1", 0), ("ln1", 0), ("k", "hot", 6), ("xhat", 0), ("k", "hot", 5),
    ("y", 1), ("splitq", 1), ("k", "hot", 7), ("scores", "ctx", 1, 0), ("v", "hot", 0, 0), ("flag",), ("tiles",),
    ("v", "hot", 1, 0), ("xhT", 0), ("v", "hot", 0, 1), ("norm", "ctx", 1, 0), ("exp", "ctx", 1, 0), ("q", 0, 0),
    ("splito", 0), ("splito", 1), ("v", "hot", 1, 1),
)
STEADY = (
    ((("q", 0, 1), ("spread", "ctx", 1)), (), (("u", 1),)),
    ((), (("gate", 1),), (("rms", 1), ("fuse", 1), ("q", 0, 2))),
    ((("x1", 1),), (("ln1", 1), ("q", 0, 3), ("xT", 2)), (("xhat", 1),)),
    ((("y", 2),), (("xhT", 1),), (("exp", "ctx", 2), ("scores", "ctx", 2), ("q", 1, 0), ("norm", "ctx", 2))),
)
LAST_BUT_ONE = (
    ((("q", 0, 2),), (("spread", "ctx", 1), ("q", 0, 1)), (("u", 1),)),
    ((), (("gate", 1),), (("rms", 1), ("fuse", 1))),
    ((("x1", 1),), (("q", 0, 3), ("ln1", 1)), (("xhat", 1),)),
    ((("x2hat", 0), ("xhT", 1)), (("split1", 0),), (("q", 1, 0), ("split1", 1))),
)
LAST = (
    ((), (("q", 0, 1), ("x2hat", 1), ("h2T", 0, 0)), ()),
    ((), (("h2T", 0, 1),), (("q", 0, 2),)),
    ((), (("x2hat", 2), ("q", 0, 3)), ()),
    ((), (), (("split2", 0),)),
)
LATE_VALUES = {(0, 0): (2,), (2, 3): (3,)}
TAIL = (
    ("ff1", 0, 0), ("spread", "last"), ("wo", 2), ("ff1", 0, 1), ("ff1", 0, 2), ("av", "last"), ("ff1", 0, 4),
    ("ff1", 0, 3), ("wo", 3), ("ln2", 3), ("split2", 1), ("ff1", 0, 5), ("ff1", 0, 6), ("x2hat", 3), ("ff1", 0, 7),
    ("h2T", 1, 0), ("ff2", 0, 0), ("ff2", 0, 1), ("ff2", 0, 2), ("h2T", 1, 1), ("ff2", 0, 3), ("ff1", 1, 0),
    ("ff1", 1, 1), ("ff1", 1, 2), ("ff1", 1, 3), ("ff1", 1, 4), ("ff1", 1, 5), ("ff1", 1, 6), ("ff1", 1, 7),
    ("ff2", 1, 0), ("ff2", 1, 1), ("ff2", 1, 2), ("ff2", 1, 3),
)



def gated_attention_block(nc, x, ctx_in, mask, w_mem, w_gate, b_gate, norm_w, lnq_g, lnq_b, wq, wkv, wo,
                          attn_gate, lnf_g, lnf_b, w1, w2, ff_gate, out):
    B, N, D = x.shape
    M, E = ctx_in.shape[1:]
    INNER = wq.shape[1]
    FF = w1.shape[1]
    DH = 64
    H = INNER // DH
    T = N // P
    KT = M // P
    K = D // P
    PAIRS = H // 2
    FM = FF // P
    HOT = KT - 1
    assert (T, KT, K, DH * 2, D, E) == (2, 4, 2, P, 2 * P, P)

    def body(nt):
        units = 4 * nt

        def between(b, slot):
            table = STEADY if b + 2 < B else LAST_BUT_ONE if b + 1 < B else LAST
            for stages in table[slot]:
                placed = []
                for st in stages:
                    if st[1] == "ctx":
                        placed.append((st[0], "ctx", b + st[2], 0))
                    elif st[0] in ("x2hat", "h2T", "split1", "split2"):
                        placed.append(st)
                    else:
                        placed.append((st[0], b + st[1]) + st[2:])
                yield placed

        held = None
        owed = None

        for b in range(B):
            if nt > 1:
                if held:
                    yield ("spread", "head", *held)
                    if owed:
                        yield ("wo", *owed)
                    yield ("av", *held)
                    owed, held = (held[0], held[1] // nt), None
                for pair in range(PAIRS):
                    yield ("k", b, pair)
                for s in range(KT):
                    yield ("v", b, s, 0)
                    yield ("v", b, s, 1)
            for u in range(units):
                slot = u // nt
                first, before, after = between(b, slot) if u % nt == (0 if slot == 0 else nt - 1) else ([], [], [])
                if nt == 1:
                    for s in LATE_VALUES.get((b, slot), ()):
                        before += [("v", "hot", s, 0), ("v", "hot", s, 1)]
                if held:
                    yield ("spread", "head", *held)
                yield ("scores", "head", b, u)
                yield ("exp", "head", b, u)
                projected, owed = owed, None
                if projected:
                    yield ("wo", *projected)
                yield from first
                yield ("norm", "head", b, u)
                yield from before
                if held:
                    yield ("av", *held)
                    if (held[1] + 1) % nt == 0:
                        owed = (held[0], held[1] // nt)
                yield from after
                if projected and projected[1] == 3:
                    yield ("ln2", projected[0])
                held = (b, u)
        for st in TAIL:
            if st[0] == "spread":
                yield ("spread", "head", *held)
            elif st[0] == "av":
                yield ("av", *held)
            elif st[0] == "wo":
                if st[1] == 3 or owed:
                    yield ("wo", B - 1, st[1])
            else:
                yield st

    with ExitStack() as stack:
        def sb(name, shape, dt=F32):
            return stack.enter_context(nc.sbuf_tensor(name, shape, dt))

        def sem(name):
            return stack.enter_context(nc.semaphore(name))

        def psum(name, shape):
            return stack.enter_context(nc.psum_tensor(name, shape, F32))

        ident = sb("ident", [P, P])
        ones_rows = sb("ones_rows", [2, P])
        ones_bf = sb("ones_bf", [1, P], BF16)
        mask_u8 = sb("mask_u8", [1, B * M], U8)
        mask_bias = sb("mask_bias", [1, B * M], BF16)
        mask_tiles = sb("mask_tiles", [B * KT, P], U8)
        tile_any = sb("tile_any", [B * KT, 1])
        flag_work = sb("flag_work", [1, 4 * B])
        short_flag = sb("short_flag", [1, 1], I32)
        x_sb = sb("x_sb", [P, B * T, D])
        ctx_start = nc.sbuf_base
        ctx_sb = sb("ctx_sb", [P, B * KT, E])
        ctxT = sb("ctxT", [P, B, M])
        wmem_sb = sb("wmem_sb", [P, K, E])
        wmem_pair = sb("wmem_pair", [P, 2, K, E], F32R)
        gate_start = nc.sbuf_base
        gate_xT_pair = sb("gate_xT_pair", [P, 2, K, D], F32R)
        gate_mem_pair = sb("gate_mem_pair", [P, 2, 2 * D], F32R)
        ones_r = sb("ones_r", [2, P], F32R)
        bgate_hi = sb("bgate_hi", [2, D], F32R)
        bgate_parts = sb("bgate_parts", [2, D], F32R)
        normw_sb = sb("normw_sb", [P, D])
        ln_rows = sb("ln_rows", [P, 4, D])
        gates = sb("gates", [P, 4])
        half_pow = sb("half_pow", [P, T])
        stage = sb("stage", [P, 2048])
        wkv_sb = sb("wkv_sb", [P, 2 * INNER])
        wq_pair = sb("wq_pair", [P, 2, 2048], F32R)
        wo_pair = sb("wo_pair", [P, 2, 2048], F32R)
        th = sb("th", [P, T, D])
        fused = sb("fused", [P, T, D])
        xhat = sb("xhat", [P, T, D])
        xhT_pair = sb("xhT_pair", [P, 2, K, N], F32R)
        stats = sb("stats", [P, T, 6])
        mean_var = sb("mean_var", [P, T, 2])
        mean_var2 = sb("mean_var2", [P, B * T, 2])
        sumsq = sb("sumsq", [P, T])
        ms = sb("ms", [P, T])
        rms_r = sb("rms_r", [P, T])
        ve = sb("ve", [P, T])
        rstd = sb("rstd", [P, T])
        ve2 = sb("ve2", [P, B, T])
        rstd2 = sb("rstd2", [P, B, T])
        q_sb = sb("q_sb", [P, PAIRS, N])
        RING = 4
        neg_max = sb("neg_max", [P, RING, 4])
        row_sum = sb("row_sum", [P, RING, 4])
        row_rcp = sb("row_rcp", [P, RING, 4])
        expd = sb("expd", [P, RING, BANK])
        probs = sb("probs", [P, RING, BANK])
        probsT = sb("probsT", [P, 2, 4, N])
        oT_pair = sb("oT_pair", [P, 2, 2, 2, N], F32R)

        wgate_sb = probs[:, 2:4, :]
        gate_cT = th
        bgate_rows, bgate_lo = xhat[0:2, 0, :], xhat[0:2, 1, :]

        yT = sb("yT", [P, N])
        warm = yT[:, :].bitcast(BF16)
        uT_pair = sb("uT_pair", [P, 2, N], F32R)
        l0_start = nc.sbuf_base
        xT_pair = sb("xT_pair", [P, 2, K, N], F32R)
        ctx_probsT = sb("ctx_probsT", [P, KT, N])
        k_start = nc.sbuf_base
        k_split = sb("k_split", [P, PAIRS, KT, 2, P])
        v_sb = sb("v_sb", [P, KT, INNER])
        gelu_pair = nc.alloc_sbuf_tensor_at("gelu_pair", [P, FM, 2, 2 * N], F32R, offset=k_start)
        h2T_pair = nc.alloc_sbuf_tensor_at("h2T_pair", [P, 2, K, 2 * N], F32R, offset=l0_start)
        w1_parts = [nc.alloc_sbuf_tensor_at(n, [P, 2048], F32R, offset=at)
                    for n, at in (("w1_hi", ctx_start), ("w1_lo", gate_start))]

        bank = [psum(f"bank{i}", [P, BANK]) for i in range(8)]
        GEN, PROJ, SC, SPREAD, CONTEXT = bank[0:2], bank[2], bank[3:5], bank[5:7], bank[7]

        wq_p = wq_pair[:, :, :].rearrange("p h (k n) -> p h k n", k=K)
        w1_p = [part[:, :].rearrange("p (k n) -> p k n", k=K) for part in w1_parts]
        w2_p = wq_pair[:, :, :].rearrange("p h (i n) -> p h i n", n=D)
        wo_p = wo_pair[:, :, :].rearrange("p h (i n) -> p h i n", n=D)

        x_in = [sem(f"x_in{b}") for b in range(B)]
        ctx_arrived = [sem("ctx_first_in"), sem("ctx_rest_in")]
        w_in = {n: sem(f"{n}_in") for n in ("mask", "wmem", "wgate", "bgate", "normw", "ln", "gates", "wkv",
                                            "wq", "wo", "w1", "w2")}
        const_ready = sem("const_ready")
        flag_ready = sem("flag_ready")
        warm_ready = sem("warm_ready")
        flag_step = sem("flag_step")
        pool_step = sem("pool_step")
        gates_ready = sem("gates_ready")
        out_done = sem("out_done")
        pe = {k: sem(f"pe_{k}") for k in ("xT", "ctxT", "gatew", "gatem", "mask", "y", "scores", "spread",
                                          "u", "gate", "xhT", "k", "v", "q", "av", "wo", "h2T", "ff1", "ff2")}
        act = {k: sem(f"act_{k}") for k in ("xT", "y", "exp", "spread", "u", "tanh", "square", "xhT", "k", "v", "o",
                                            "h2T", "gelu", "geluhi", "wsplit", "gatew", "wmem", "bgate", "mask")}
        dve = {k: sem(f"dve_{k}") for k in ("xT", "u", "ctxT", "gatew", "wmem", "bgate", "negmax", "rcp", "spread",
                                            "gated", "ms", "ve", "xhat", "xhT", "k", "v", "q", "o", "wo",
                                            "ve2", "x2hat", "h2T", "gelu", "out", "wsplit", "mask")}
        pool = {k: sem(f"pool_{k}") for k in ("rms", "rstd", "probs", "rstd2", "wsplit", "scaled", "affine")}

        PRO = list(PROLOGUE)
        plans = {nt: PRO + list(body(nt)) for nt in (1, KT)}

        def counts(nt):
            seen, place = {}, {}
            for st in plans[nt]:
                seen[st[0]] = seen.get(st[0], 0) + 1
                place[st] = seen[st[0]]
            return place

        class Path:

            def __init__(self, nt):
                self.nt = nt
                self.plan = plans[nt]
                self.at = counts(nt)
                self.units = 4 * nt
                self.heads = 4 // nt
                self.uses = []
                self.use, last_use, turn = {}, {}, 0
                for at, st in enumerate(self.plan):
                    n = {"xT": 1, "ctxT": 1, "weights": 4, "tiles": 1, "y": 1, "u": 1, "gate": 2, "xhT": 1, "k": 1,
                         "v": 1, "q": 1, "h2T": 1, "ff1": 1, "ff2": 1}.get(st[0], 0)
                    banks = GEN + [PROJ, CONTEXT] if at < len(PRO) else GEN
                    for i in range(n):
                        here = banks[turn % len(banks)]
                        self.use[(st, i)] = len(self.uses)
                        self.uses.append((here, last_use.get(here.name)))
                        last_use[here.name] = (st, i)
                        turn += 1
                self.last_use = last_use
                self.all_scores = T * sum(st[0] == "scores" for st in self.plan)
                assert self.all_scores % RING == 0

            def bank(self, st, i=0):
                return self.uses[self.use[(st, i)]][0]

            def bank_free(self, st, i=0):
                before = self.uses[self.use[(st, i)]][1]
                return self.was_read(*before) if before else []

            def was_read(self, old, j):
                c = self.at[old]
                return {
                    "xT": [(dve["xT"], c)], "ctxT": [(dve["ctxT"], c)], "weights": [(dve["gatew"], j + 1)],
                    "tiles": [(flag_ready, 1)],
                    "y": [(act["y"], c)], "u": [(dve["u"], c)], "gate": [(dve["gated"], T * (c - 1) + j + 1)],
                    "xhT": [(dve["xhT"], c)], "k": [(dve["k"], c), (act["k"], c)],
                    "v": [(act["v"], (c + 1) // 2)] if c % 2 else [(dve["v"], c // 2)],
                    "q": [(dve["q"], c)], "h2T": [(dve["h2T"], c)],
                    "ff1": [(act["gelu"], c)], "ff2": [(dve["out"], c)],
                }[old[0]]

            def score_no(self, kind, b, u, t):
                return T * (self.at[("scores", kind, b, u)] - 1) + t

            @staticmethod
            def split_no(st):
                return 2 * ("splitq", "splito", "split1", "split2").index(st[0]) + st[1] + 1

            def last_unit(self, pair):
                return (2 * pair + 1) // self.heads

            def quads(self, b, u):
                return 4 * b + (u + 1) // self.nt

            def keys_of(self, b):
                return "hot" if self.nt == 1 else b

        paths = {nt: Path(nt) for nt in (1, KT)}

        def cols_of(st):
            return slice(st[1] * 1024, (st[1] + 1) * 1024)

        def split_matmul(bank_ap, lhs, rhs, start, stop):
            for n, (a, c) in enumerate(((HI, HI), (HI, LO), (LO, HI))):
                last = nc.tensor.matmul(bank_ap, lhs(a), rhs(c), start=start and n == 0, stop=stop and n == 2)
            return last

        def spread_to(eng, path, st, t):
            kind, b, u = st[1:]
            if kind == "ctx":
                if b:
                    eng.wait_ge(pe["u"], b)
                return ctx_probsT[:, :, t * P:(t + 1) * P]
            unit = b * path.units + u
            if unit >= 2:
                eng.wait_ge(pe["av"], unit - 1)
            return probsT[:, unit % 2, :, t * P:(t + 1) * P]

        def x2hat_buf(b):
            return xhat if b % 2 else fused

        def mem_view(part):
            return gate_mem_pair[:, part, D:2 * D].rearrange("e (p k) -> e k p", k=K)

        def mem_bank(bank_ap):
            return bank_ap[:, 0:D].rearrange("e (k p) -> e k p", k=K)

        block = stack.enter_context(nc.Block())

        @block.sync
        def _(sp):
            def load(dst, src, s):
                sp.dma_start(dst, src).then_inc(s, 16)

            def load_x(b):
                load(x_sb[:, b * T:(b + 1) * T, :], x[b].rearrange("(t p) d -> p t d", p=P), x_in[b])

            load_x(0)
            load(wmem_sb[:, :, :], w_mem.rearrange("(p k) e -> p k e", k=K), w_in["wmem"])
            load(wgate_sb, w_gate.rearrange("(k p) f -> p k f", p=P), w_in["wgate"])
            load(bgate_rows, b_gate.rearrange("(a d) -> a d", a=1).to_broadcast([2, D]), w_in["bgate"])
            load(ctx_sb[:, KT:B * KT, :], ctx_in[1:B].rearrange("b (t p) e -> p (b t) e", p=P), ctx_arrived[1])
            load(wkv_sb[:, :], wkv, w_in["wkv"])
            load(mask_tiles[:, :], mask.rearrange("b (t n) -> (b t) n", n=P), w_in["mask"])
            load(mask_u8[:, :], mask.rearrange("(a b) m -> a (b m)", a=1), w_in["mask"])
            load(stage[:, :].rearrange("p (k n) -> p k n", k=K), wq.rearrange("(p k) n -> p k n", k=K), w_in["wq"])
            load_x(1)
            load(normw_sb[:, :], norm_w.rearrange("(a d) -> a d", a=1).to_broadcast([P, D]), w_in["normw"])
            with nc.allow_non_contiguous_dma(reason="single values"):
                for i, v in enumerate((attn_gate, ff_gate)):
                    load(gates[:, i:i + 1], v.rearrange("(a c) -> a c", a=1).to_broadcast([P, 1]), w_in["gates"])
            for i, v in enumerate((lnq_g, lnq_b, lnf_g, lnf_b)):
                load(ln_rows[:, i, :], v.rearrange("(a d) -> a d", a=1).to_broadcast([P, D]), w_in["ln"])
            for b in range(2, B):
                load_x(b)
            sp.wait_ge(act["wsplit"], 2)
            sp.wait_ge(dve["wsplit"], 2)
            load(stage[:, :].rearrange("p (i n) -> p i n", n=D), wo.rearrange("(i p) n -> p i n", p=P), w_in["wo"])
            sp.wait_ge(act["wsplit"], 4)
            sp.wait_ge(pool["wsplit"], 2)
            load(stage[:, :].rearrange("p (k n) -> p k n", k=K), w1.rearrange("(p k) n -> p k n", k=K), w_in["w1"])
            sp.wait_ge(act["wsplit"], 6)
            sp.wait_ge(dve["wsplit"], 4)
            load(stage[:, :].rearrange("p (i n) -> p i n", n=D), w2.rearrange("(i p) n -> p i n", p=P), w_in["w2"])
            for b in range(B):
                for t in range(T):
                    sp.wait_ge(dve["out"], b * T + t + 1)
                    sp.dma_start(out[b, t * P:(t + 1) * P, :], x_sb[:, b * T + t, :]).then_inc(out_done, 16)
            sp.wait_ge(out_done, 16 * B * T)

        @block.gpsimd
        def _(gp):
            nc.gpsimd.memset(ident[:, :], 0.0).then_inc(pool_step, 1)
            nc.gpsimd.memset(ones_rows[:, :], 1.0).then_inc(const_ready, 1)
            nc.gpsimd.memset(ones_bf[:, :], 1.0).then_inc(const_ready, 1)
            gp.wait_ge(pool_step, 1)
            nc.gpsimd.affine_select(out=ident[:, :], in_=ident[:, :], compare_op=ALU.not_equal, fill=1.0, base=0,
                                    pattern=[[-1, P]], channel_multiplier=1).then_inc(const_ready, 1)
            nc.gpsimd.memset(half_pow[:, :], -0.5).then_inc(const_ready, 1)
            nc.gpsimd.memset(k_split[0:DH, :, :, 1, :], 0.0).then_inc(const_ready, 1)
            gp.wait_ge(const_ready, 5)
            nc.gpsimd.memset(k_split[DH:P, :, :, 0, :], 0.0).then_inc(const_ready, 1)

            def run(path, plan):
                for st in plan:
                    c = path.at[st]
                    if st[0] == "norm":
                        for t in range(T):
                            n = path.score_no(*st[1:], t)
                            r, hb = n % RING, (path.heads if st[1] == "head" else 1)
                            gp.wait_ge(dve["rcp"], n + 1)
                            if n >= RING:
                                gp.wait_ge(pe["spread"], n - RING + 1)
                            nc.gpsimd.tensor_tensor(
                                probs[:, r, :].rearrange("p (h k) -> p h k", h=hb),
                                expd[:, r, :].rearrange("p (h k) -> p h k", h=hb),
                                row_rcp[:, r, 0:hb].rearrange("p (h k) -> p h k", k=1).to_broadcast(
                                    [P, hb, BANK // hb]),
                                ALU.mult).then_inc(pool["probs"], 1)
                    elif st[0] == "rms":
                        gp.wait_ge(dve["ms"], c)
                        if c > 1:
                            gp.wait_ge(dve["ve"], c - 1)
                        nc.gpsimd.tensor_tensor(rms_r[:, :], ms[:, :], half_pow[:, :], ALU.pow
                                                ).then_inc(pool["rms"], 1)
                    elif st[0] == "ln1":
                        gp.wait_ge(dve["ve"], c)
                        if c > 1:
                            gp.wait_ge(dve["xhat"], c - 1)
                        nc.gpsimd.tensor_tensor(rstd[:, :], ve[:, :], half_pow[:, :], ALU.pow
                                                ).then_inc(pool["rstd"], 1)
                    elif st[0] == "ln2":
                        gp.wait_ge(dve["ve2"], c)
                        nc.gpsimd.tensor_tensor(rstd2[:, st[1], :], ve2[:, st[1], :], half_pow[:, :], ALU.pow
                                                ).then_inc(pool["rstd2"], 1)
                    elif st[0] in ("xhat", "x2hat"):
                        ln = 0 if st[0] == "xhat" else 2
                        n = path.at[st] if ln == 0 else B + path.at[st]
                        gp.wait_ge(dve[st[0]], c)
                        if n == 1:
                            gp.wait_ge(w_in["ln"], 64)
                        normed = x2hat_buf(st[1]) if ln else xhat
                        row = ln_rows[:, ln:ln + 2, :].rearrange("p (i a) d -> p i a d", a=1)
                        nc.gpsimd.tensor_tensor(normed[:, :, :], normed[:, :, :], row[:, 0].to_broadcast([P, T, D]),
                                                ALU.mult).then_inc(pool["scaled"], 1)
                        gp.wait_ge(pool["scaled"], n)
                        nc.gpsimd.tensor_tensor(normed[:, :, :], normed[:, :, :], row[:, 1].to_broadcast([P, T, D]),
                                                ALU.add).then_inc(pool["affine"], 1)
                    elif st[0] == "splito":
                        gp.wait_ge(act["wsplit"], path.split_no(st))
                        nc.gpsimd.tensor_tensor(wo_pair[:, LO, cols_of(st)], stage[:, cols_of(st)],
                                                wo_pair[:, HI, cols_of(st)].bitcast(F32), ALU.subtract
                                                ).then_inc(pool["wsplit"], 1)

            gp.wait_ge(const_ready, 6)
            run(paths[1], PRO)
            gp.wait_ge(flag_ready, 1)
            short = gp.value_load(short_flag[0:1, 0:1], min_val=0, max_val=1)
            with gp.If(short == 1):
                run(paths[1], paths[1].plan[len(PRO):])
            with gp.Else():
                run(paths[KT], paths[KT].plan[len(PRO):])

        @block.scalar
        def _(sc):
            sc.dma_start(ctx_sb[:, 0:KT, :], ctx_in[0].rearrange("(t p) e -> p t e", p=P)).then_inc(ctx_arrived[0], 16)

            def run(path, plan):
                for st in plan:
                    kind, c = st[0], path.at[st]
                    if kind == "xT":
                        b = st[1]
                        sc.wait_ge(pe["xT"], c)
                        if b:
                            sc.wait_ge(pe["gate"], T * b)
                        nc.scalar.copy(xT_pair[:, HI, :, :], path.bank(st)[:, :].rearrange("p (k n) -> p k n", k=K)
                                       ).then_inc(act["xT"], 1)
                    elif kind == "mask":
                        sc.wait_ge(w_in["mask"], 32)
                        nc.scalar.activation(mask_bias[:, :], mask_u8[:, :], ACT.Copy, scale=-MASKED, bias=MASKED
                                             ).then_inc(act["mask"], 1)
                    elif kind == "wmem":
                        sc.wait_ge(w_in["wmem"], 16)
                        nc.scalar.copy(wmem_pair[:, HI, :, :], wmem_sb[:, :, :]).then_inc(act["wmem"], 1)
                    elif kind == "weights":
                        sc.wait_ge(pe["gatew"], 1)
                        nc.scalar.copy(gate_xT_pair[:, HI, :, :],
                                       path.bank(st, 0)[:, :].rearrange("p (k n) -> p k n", k=K)
                                       ).then_inc(act["gatew"], 1)
                        sc.wait_ge(pe["gatew"], 3)
                        nc.scalar.copy(mem_view(HI), mem_bank(path.bank(st, 2))).then_inc(act["gatew"], 1)
                        sc.wait_ge(pe["gatem"], 1)
                        nc.scalar.copy(gate_mem_pair[:, HI, 0:D], path.bank(st, 3)[:, 0:D]).then_inc(act["gatew"], 1)
                        sc.wait_ge(w_in["bgate"], 16)
                        nc.scalar.copy(bgate_hi[:, :], bgate_rows).then_inc(act["bgate"], 1)
                    elif kind == "ln1" and c == 1:
                        sc.wait_ge(w_in["gates"], 32)
                        nc.scalar.activation(gates[:, 2:4], gates[:, 0:2], ACT.Tanh).then_inc(gates_ready, 1)
                    elif kind == "y":
                        sc.wait_ge(pe["y"], c)
                        if c > 1:
                            sc.wait_ge(pe["scores"], path.score_no("ctx", st[1] - 1, 0, T - 1) + 1)
                        nc.scalar.activation(yT[:, :], path.bank(st)[:, 0:N], ACT.Copy, scale=D ** -0.5
                                             ).then_inc(act["y"], 1)
                    elif kind == "exp":
                        for t in range(T):
                            n = path.score_no(*st[1:], t)
                            r, hb = n % RING, (path.heads if st[1] == "head" else 1)
                            sc.wait_ge(dve["negmax"], n + 1)
                            if n >= RING:
                                sc.wait_ge(pool["probs"], n - RING + 1)
                            w = BANK // hb
                            for h in range(hb):
                                last = nc.scalar.activation(
                                    expd[:, r, h * w:(h + 1) * w], SC[n % 2][:, h * w:(h + 1) * w], ACT.Exp,
                                    bias=neg_max[:, r, h:h + 1], accum_out=row_sum[:, r, h:h + 1])
                            last.then_inc(act["exp"], 1)
                    elif kind == "spread":
                        n = path.score_no(*st[1:], 0)
                        sc.wait_ge(pe["spread"], n + 1)
                        nc.scalar.copy(spread_to(sc, path, st, 0),
                                       SPREAD[n % 2][:, :].rearrange("p (j n) -> p j n", j=4)
                                       ).then_inc(act["spread"], 1)
                    elif kind == "u":
                        sc.wait_ge(pe["u"], c)
                        if c > 1:
                            sc.wait_ge(pe["gate"], T * (c - 1))
                        nc.scalar.copy(uT_pair[:, HI, :], path.bank(st)[:, 0:N]).then_inc(act["u"], 1)
                    elif kind == "gate":
                        for t in range(T):
                            sc.wait_ge(pe["gate"], T * (c - 1) + t + 1)
                            if c > 1:
                                sc.wait_ge(act["square"], c - 1)
                            nc.scalar.activation(th[:, t, :], path.bank(st, t)[:, 0:D], ACT.Tanh, scale=0.5
                                                 ).then_inc(act["tanh"], 1)
                    elif kind == "fuse":
                        for t in range(T):
                            sc.wait_ge(dve["gated"], T * (c - 1) + t + 1)
                            last = nc.scalar.activation(th[:, t, :], fused[:, t, :], ACT.Square,
                                                        accum_out=sumsq[:, t:t + 1])
                        last.then_inc(act["square"], 1)
                    elif kind == "xhT":
                        sc.wait_ge(pe["xhT"], c)
                        if c > 1:
                            sc.wait_ge(pe["q"], path.at[("q", st[1] - 1, 3)])
                        nc.scalar.copy(xhT_pair[:, HI, :, :], path.bank(st)[:, :].rearrange("p (k n) -> p k n", k=K)
                                       ).then_inc(act["xhT"], 1)
                    elif kind == "k":
                        sc.wait_ge(pe["k"], c)
                        if c > PAIRS:
                            sc.wait_ge(act["k"], c - PAIRS)
                        nc.scalar.copy(k_split[0:DH, st[2], :, 0, :],
                                       path.bank(st)[0:DH, :].rearrange("p (s n) -> p s n", s=KT)
                                       ).then_inc(act["k"], 1)
                    elif kind == "v" and st[3] == 0:
                        sc.wait_ge(pe["v"], c)
                        if c > 1:
                            sc.wait_ge(act["v"], (c + 1) // 2 - 1)
                        nc.scalar.copy(v_sb[:, st[2], 0:BANK], path.bank(st)[:, :]).then_inc(act["v"], 1)
                    elif kind == "av":
                        b, u = st[1:]
                        if (u + 1) % path.nt == 0:
                            g = path.quads(b, u)
                            sc.wait_ge(pe["av"], c)
                            if g > 2:
                                sc.wait_ge(pe["wo"], g - 2)
                            nc.scalar.copy(oT_pair[:, HI, (g - 1) % 2, :, :],
                                           CONTEXT[:, :].rearrange("p (j n) -> p j n", j=2)).then_inc(act["o"], 1)
                    elif kind == "splitq":
                        sc.wait_ge(w_in["wq"], 16)
                        nc.scalar.activation(wq_pair[:, HI, cols_of(st)], stage[:, cols_of(st)], ACT.Copy,
                                             scale=DH ** -0.5).then_inc(act["wsplit"], 1)
                    elif kind == "splito":
                        sc.wait_ge(w_in["wo"], 16)
                        nc.scalar.copy(wo_pair[:, HI, cols_of(st)], stage[:, cols_of(st)]).then_inc(act["wsplit"], 1)
                    elif kind == "split1":
                        sc.wait_ge(w_in["w1"], 16)
                        sc.wait_ge(pe["u"], B)
                        nc.scalar.copy(w1_parts[HI][:, cols_of(st)], stage[:, cols_of(st)]).then_inc(act["wsplit"], 1)
                    elif kind == "split2":
                        sc.wait_ge(w_in["w2"], 16)
                        sc.wait_ge(pe["q"], path.at[("q", B - 1, 3)])
                        nc.scalar.copy(wq_pair[:, HI, cols_of(st)], stage[:, cols_of(st)]).then_inc(act["wsplit"], 1)
                    elif kind == "h2T":
                        f, half = st[1:]
                        sc.wait_ge(pe["h2T"], c)
                        if f:
                            sc.wait_ge(pe["ff1"], FM * f)
                        else:
                            sc.wait_ge(pe["gate"], T * B)
                        nc.scalar.copy(h2T_pair[:, HI, :, half * N:(half + 1) * N],
                                       path.bank(st)[:, :].rearrange("p (k n) -> p k n", k=K)
                                       ).then_inc(act["h2T"], 1)
                    elif kind == "ff1":
                        f, m = st[1:]
                        sc.wait_ge(pe["ff1"], c)
                        if c > RING:
                            sc.wait_ge(dve["gelu"], c - RING)
                        else:
                            sc.wait_ge(pool["probs"], path.all_scores - RING + c)
                        nc.scalar.activation(expd[:, (c - 1) % RING, :], path.bank(st)[:, :], ACT.Gelu
                                             ).then_inc(act["gelu"], 1)
                        if f:
                            sc.wait_ge(pe["ff2"], 2 * T * f)
                        elif m == 0:
                            sc.wait_ge(pe["scores"], path.all_scores)
                        sc.wait_ge(act["gelu"], c)
                        nc.scalar.copy(gelu_pair[:, m, HI, :], expd[:, (c - 1) % RING, :]).then_inc(act["geluhi"], 1)

            sc.wait_ge(const_ready, 1)
            nc.scalar.copy(ones_r[:, :], ones_rows[:, :]).then_inc(act["bgate"], 1)
            run(paths[1], PRO)
            sc.wait_ge(flag_ready, 1)
            short = sc.value_load(short_flag[0:1, 0:1], min_val=0, max_val=1)
            with sc.If(short == 1):
                run(paths[1], paths[1].plan[len(PRO):])
            with sc.Else():
                run(paths[KT], paths[KT].plan[len(PRO):])

        @block.vector
        def _(ve_):
            def chain(ins):
                flag_count[0] += 1
                ins.then_inc(flag_step, 1)
                ve_.wait_ge(flag_step, flag_count[0])

            flag_count = [0]

            def tile_stats(b):
                for t in range(T):
                    last = nc.vector.bn_stats(stats[:, t, :], x_sb[:, b * T + t, :])
                chain(last)

            def aggregate(dst, at):
                for t in range(T):
                    last = nc.vector.bn_aggr(dst[:, at + t, :], stats[:, t, :])
                chain(last)

            def run(path, plan):
                for st in plan:
                    kind, c = st[0], path.at[st]
                    if kind == "xT":
                        ve_.wait_ge(act["xT"], c)
                        nc.vector.tensor_tensor(xT_pair[:, LO, :, :],
                                                path.bank(st)[:, :].rearrange("p (k n) -> p k n", k=K),
                                                xT_pair[:, HI, :, :].bitcast(F32), ALU.subtract
                                                ).then_inc(dve["xT"], 1)
                    elif kind == "u":
                        ve_.wait_ge(act["u"], c)
                        nc.vector.tensor_tensor(uT_pair[:, LO, :], path.bank(st)[:, 0:N],
                                                uT_pair[:, HI, :].bitcast(F32), ALU.subtract).then_inc(dve["u"], 1)
                    elif kind == "ctxT":
                        ve_.wait_ge(pe["ctxT"], c)
                        nc.vector.tensor_copy(ctxT[:, st[1], :], path.bank(st)[:, :]).then_inc(dve["ctxT"], 1)
                    elif kind == "weights":
                        ve_.wait_ge(act["gatew"], 1)
                        nc.vector.tensor_tensor(gate_xT_pair[:, LO, :, :],
                                                path.bank(st, 0)[:, :].rearrange("p (k n) -> p k n", k=K),
                                                gate_xT_pair[:, HI, :, :].bitcast(F32), ALU.subtract
                                                ).then_inc(dve["gatew"], 1)
                        ve_.wait_ge(pe["gatew"], 2)
                        nc.vector.tensor_copy(gate_cT[:, :, :],
                                              path.bank(st, 1)[:, :].rearrange("p (k n) -> p k n", k=K)
                                              ).then_inc(dve["gatew"], 1)
                        ve_.wait_ge(act["gatew"], 2)
                        nc.vector.tensor_tensor(mem_view(LO), mem_bank(path.bank(st, 2)),
                                                mem_view(HI).bitcast(F32), ALU.subtract).then_inc(dve["gatew"], 1)
                        ve_.wait_ge(act["gatew"], 3)
                        nc.vector.tensor_tensor(gate_mem_pair[:, LO, 0:D], path.bank(st, 3)[:, 0:D],
                                                gate_mem_pair[:, HI, 0:D].bitcast(F32), ALU.subtract
                                                ).then_inc(dve["gatew"], 1)
                        ve_.wait_ge(act["bgate"], 2)
                        chain(nc.vector.tensor_tensor(bgate_lo, bgate_rows, bgate_hi[:, :].bitcast(F32),
                                                      ALU.subtract))
                        chain(nc.vector.tensor_scalar(bgate_lo, bgate_lo, ident[0:2, 1:2], None, ALU.mult))
                        nc.vector.scalar_tensor_tensor(bgate_parts[:, :], bgate_hi[:, :].bitcast(F32),
                                                       ident[0:2, 0:1], bgate_lo, ALU.mult, ALU.add
                                                       ).then_inc(dve["bgate"], 1)
                    elif kind == "mask":
                        ve_.wait_ge(w_in["mask"], 32)
                        nc.vector.reduce_max(tile_any[:, :], mask_tiles[:, :], AX_X).then_inc(dve["mask"], 1)
                    elif kind == "flag":
                        ve_.wait_ge(pe["mask"], 1)
                        any_v = path.bank(("tiles",))[0:1, 0:B * KT].rearrange("a (b t) -> a b t", t=KT)
                        chain(nc.vector.reduce_max(flag_work[:, 0:B], any_v[:, :, 0:HOT], AX_X))
                        chain(nc.vector.tensor_scalar(flag_work[:, B:2 * B], flag_work[:, 0:B], -1.0, 1.0,
                                                      ALU.mult, ALU.add))
                        chain(nc.vector.tensor_tensor(flag_work[:, 2 * B:3 * B], flag_work[:, B:2 * B],
                                                      any_v[:, :, HOT], ALU.mult))
                        nc.vector.tensor_reduce(short_flag[:, :], flag_work[:, 2 * B:3 * B], AX_X, ALU.min
                                                ).then_inc(flag_ready, 1)
                    elif kind == "wmem":
                        ve_.wait_ge(act["wmem"], 1)
                        nc.vector.tensor_tensor(wmem_pair[:, LO, :, :], wmem_sb[:, :, :],
                                                wmem_pair[:, HI, :, :].bitcast(F32), ALU.subtract
                                                ).then_inc(dve["wmem"], 1)
                    elif kind == "scores":
                        for t in range(T):
                            n = path.score_no(*st[1:], t)
                            r, hb = n % RING, (path.heads if st[1] == "head" else 1)
                            ve_.wait_ge(pe["scores"], n + 1)
                            nc.vector.tensor_reduce(neg_max[:, r, 0:hb],
                                                    SC[n % 2][:, :].rearrange("p (h k) -> p h k", h=hb),
                                                    AX_X, ALU.max, negate=True).then_inc(dve["negmax"], 1)
                    elif kind == "norm":
                        for t in range(T):
                            n = path.score_no(*st[1:], t)
                            r, hb = n % RING, (path.heads if st[1] == "head" else 1)
                            ve_.wait_ge(act["exp"], n + 1)
                            nc.vector.reciprocal(row_rcp[:, r, 0:hb], row_sum[:, r, 0:hb]).then_inc(dve["rcp"], 1)
                    elif kind == "spread":
                        n = path.score_no(*st[1:], 1)
                        ve_.wait_ge(pe["spread"], n + 1)
                        nc.vector.tensor_copy(spread_to(ve_, path, st, 1),
                                              SPREAD[n % 2][:, :].rearrange("p (j n) -> p j n", j=4)
                                              ).then_inc(dve["spread"], 1)
                    elif kind == "gate":
                        for t in range(T):
                            ve_.wait_ge(act["tanh"], T * (c - 1) + t + 1)
                            if c > 1:
                                ve_.wait_ge(act["square"], c - 1)
                            chain(nc.vector.scalar_tensor_tensor(
                                fused[:, t, :], th[:, t, :], 1.0, path.bank(st, t)[:, D:2 * D], ALU.add, ALU.mult))
                            gated = nc.vector.scalar_tensor_tensor(
                                fused[:, t, :], fused[:, t, :], 0.5, x_sb[:, st[1] * T + t, :], ALU.mult, ALU.add)
                            gated.then_inc(dve["gated"], 1)
                    elif kind == "rms":
                        ve_.wait_ge(act["square"], c)
                        nc.vector.tensor_scalar(ms[:, :], sumsq[:, :], 1.0 / D, RMS_EPS, ALU.mult, ALU.add
                                                ).then_inc(dve["ms"], 1)
                    elif kind == "x1":
                        b = st[1]
                        ve_.wait_ge(pool["rms"], c)
                        if c == 1:
                            ve_.wait_ge(w_in["normw"], 16)
                        for t in range(T):
                            last = nc.vector.scalar_tensor_tensor(
                                x_sb[:, b * T + t, :], fused[:, t, :], rms_r[:, t:t + 1], normw_sb[:, :],
                                ALU.mult, ALU.mult)
                        chain(last)
                        tile_stats(b)
                    elif kind == "ln1":
                        aggregate(mean_var, 0)
                        nc.vector.tensor_scalar(ve[:, :], mean_var[:, :, 1], LN_EPS, None, ALU.add
                                                ).then_inc(dve["ve"], 1)
                    elif kind == "xhat":
                        b = st[1]
                        ve_.wait_ge(pool["rstd"], c)
                        if c > 1:
                            ve_.wait_ge(pe["xhT"], c - 1)
                        for t in range(T):
                            last = nc.vector.tensor_scalar(xhat[:, t, :], x_sb[:, b * T + t, :], mean_var[:, t, 0:1],
                                                           rstd[:, t:t + 1], ALU.subtract, ALU.mult)
                        last.then_inc(dve["xhat"], 1)
                    elif kind == "xhT":
                        ve_.wait_ge(act["xhT"], c)
                        nc.vector.tensor_tensor(xhT_pair[:, LO, :, :],
                                                path.bank(st)[:, :].rearrange("p (k n) -> p k n", k=K),
                                                xhT_pair[:, HI, :, :].bitcast(F32), ALU.subtract
                                                ).then_inc(dve["xhT"], 1)
                    elif kind == "k":
                        ve_.wait_ge(pe["k"], c)
                        if c > PAIRS:
                            ve_.wait_ge(dve["k"], c - PAIRS)
                        nc.vector.tensor_copy(k_split[DH:P, st[2], :, 1, :],
                                              path.bank(st)[DH:P, :].rearrange("p (s n) -> p s n", s=KT)
                                              ).then_inc(dve["k"], 1)
                    elif kind == "v" and st[3] == 1:
                        ve_.wait_ge(pe["v"], c)
                        if c > 2:
                            ve_.wait_ge(dve["v"], c // 2 - 1)
                        nc.vector.tensor_copy(v_sb[:, st[2], BANK:2 * BANK], path.bank(st)[:, :]).then_inc(dve["v"], 1)
                    elif kind == "q":
                        b, j = st[1:]
                        ve_.wait_ge(pe["q"], c)
                        if b:
                            ve_.wait_ge(pe["scores"],
                                        path.score_no("head", b - 1, path.last_unit(2 * j + 1), T - 1) + 1)
                        nc.vector.tensor_copy(q_sb[:, 2 * j:2 * j + 2, :],
                                              path.bank(st)[:, :].rearrange("p (i n) -> p i n", i=2)
                                              ).then_inc(dve["q"], 1)
                    elif kind == "av":
                        b, u = st[1:]
                        if (u + 1) % path.nt == 0:
                            g = path.quads(b, u)
                            ve_.wait_ge(act["o"], g)
                            nc.vector.tensor_tensor(oT_pair[:, LO, (g - 1) % 2, :, :],
                                                    CONTEXT[:, :].rearrange("p (j n) -> p j n", j=2),
                                                    oT_pair[:, HI, (g - 1) % 2, :, :].bitcast(F32), ALU.subtract
                                                    ).then_inc(dve["o"], 1)
                    elif kind == "splitq":
                        ve_.wait_ge(act["wsplit"], path.split_no(st))
                        nc.vector.scalar_tensor_tensor(wq_pair[:, LO, cols_of(st)], stage[:, cols_of(st)], DH ** -0.5,
                                                       wq_pair[:, HI, cols_of(st)].bitcast(F32), ALU.mult, ALU.subtract
                                                       ).then_inc(dve["wsplit"], 1)
                    elif kind == "split1":
                        ve_.wait_ge(act["wsplit"], path.split_no(st))
                        ve_.wait_ge(pe["gate"], T * B)
                        nc.vector.tensor_tensor(w1_parts[LO][:, cols_of(st)], stage[:, cols_of(st)],
                                                w1_parts[HI][:, cols_of(st)].bitcast(F32), ALU.subtract
                                                ).then_inc(dve["wsplit"], 1)
                    elif kind == "split2":
                        ve_.wait_ge(act["wsplit"], path.split_no(st))
                        nc.vector.tensor_tensor(wq_pair[:, LO, cols_of(st)], stage[:, cols_of(st)],
                                                wq_pair[:, HI, cols_of(st)].bitcast(F32), ALU.subtract
                                                ).then_inc(dve["wsplit"], 1)
                    elif kind == "wo" and st[2] == 3:
                        b = st[1]
                        ve_.wait_ge(pe["wo"], c)
                        if b == 0:
                            ve_.wait_ge(gates_ready, 1)
                        nc.vector.scalar_tensor_tensor(
                            x_sb[:, b * T:b * T + T, :], PROJ[:, :].rearrange("p (t n) -> p t n", t=T),
                            gates[:, 2:3], x_sb[:, b * T:b * T + T, :], ALU.mult, ALU.add).then_inc(dve["wo"], 1)
                    elif kind == "ln2":
                        b = st[1]
                        ve_.wait_ge(dve["wo"], b + 1)
                        tile_stats(b)
                        aggregate(mean_var2, b * T)
                        nc.vector.tensor_scalar(ve2[:, b, :], mean_var2[:, b * T:b * T + T, 1], LN_EPS, None, ALU.add
                                                ).then_inc(dve["ve2"], 1)
                    elif kind == "x2hat":
                        b = st[1]
                        ve_.wait_ge(pool["rstd2"], path.at[("ln2", b)])
                        if c > 2:
                            ve_.wait_ge(pe["h2T"], c - 2)
                        elif c == 2:
                            ve_.wait_ge(pe["xhT"], B)
                        else:
                            ve_.wait_ge(act["square"], B)
                        for t in range(T):
                            last = nc.vector.tensor_scalar(x2hat_buf(b)[:, t, :], x_sb[:, b * T + t, :],
                                                           mean_var2[:, b * T + t, 0:1], rstd2[:, b, t:t + 1],
                                                           ALU.subtract, ALU.mult)
                        last.then_inc(dve["x2hat"], 1)
                    elif kind == "h2T":
                        f, half = st[1:]
                        ve_.wait_ge(act["h2T"], c)
                        nc.vector.tensor_tensor(h2T_pair[:, LO, :, half * N:(half + 1) * N],
                                                path.bank(st)[:, :].rearrange("p (k n) -> p k n", k=K),
                                                h2T_pair[:, HI, :, half * N:(half + 1) * N].bitcast(F32),
                                                ALU.subtract).then_inc(dve["h2T"], 1)
                    elif kind == "ff1":
                        f, m = st[1:]
                        ve_.wait_ge(act["geluhi"], c)
                        nc.vector.tensor_tensor(gelu_pair[:, m, LO, :], expd[:, (c - 1) % RING, :],
                                                gelu_pair[:, m, HI, :].bitcast(F32), ALU.subtract
                                                ).then_inc(dve["gelu"], 1)
                    elif kind == "ff2":
                        f, i = st[1:]
                        tile = 2 * T * f + i
                        ve_.wait_ge(pe["ff2"], c)
                        nc.vector.scalar_tensor_tensor(
                            x_sb[:, tile, :], path.bank(st)[:, 0:D], gates[:, 3:4], x_sb[:, tile, :],
                            ALU.mult, ALU.add).then_inc(dve["out"], 1)

            nc.vector.memset(warm, 0.0).then_inc(warm_ready, 1)
            run(paths[1], PRO)
            before = flag_count[0]
            ve_.wait_ge(flag_ready, 1)
            short = ve_.value_load(short_flag[0:1, 0:1], min_val=0, max_val=1)
            with ve_.If(short == 1):
                run(paths[1], paths[1].plan[len(PRO):])
            with ve_.Else():
                flag_count[0] = before
                run(paths[KT], paths[KT].plan[len(PRO):])

        @block.tensor
        def _(te):
            def free(path, st, i=0):
                for s, v in path.bank_free(st, i):
                    te.wait_ge(s, v)

            def run(path, plan):
                for st in plan:
                    kind, c = st[0], path.at[st]
                    if kind == "xT":
                        b = st[1]
                        te.wait_ge(x_in[b], 16)
                        free(path, st)
                        for k in range(K):
                            for t in range(T):
                                last = nc.tensor.transpose(path.bank(st)[:, k * N + t * P:k * N + (t + 1) * P],
                                                           x_sb[:, b * T + t, k:D:K], ident[:, :])
                        last.then_inc(pe["xT"], 1)
                    elif kind == "ctxT":
                        b = st[1]
                        te.wait_ge(ctx_arrived[min(b, 1)], 16)
                        free(path, st)
                        for j in range(KT):
                            last = nc.tensor.transpose(path.bank(st)[:, j * P:(j + 1) * P], ctx_sb[:, b * KT + j, :],
                                                       ident[:, :])
                        last.then_inc(pe["ctxT"], 1)
                    elif kind == "weights":
                        te.wait_ge(w_in["wgate"], 16)
                        for i in range(2):
                            free(path, st, i)
                            for k in range(K):
                                for dt in range(K):
                                    last = nc.tensor.transpose(
                                        path.bank(st, i)[:, k * D + dt * P:k * D + (dt + 1) * P],
                                        wgate_sb[:, dt, i * D + k:(i + 1) * D:K], ident[:, :])
                            last.then_inc(pe["gatew"], 1)
                        free(path, st, 2)
                        for k in range(K):
                            last = nc.tensor.transpose(path.bank(st, 2)[:, k * P:(k + 1) * P], wmem_sb[:, k, :],
                                                       ident[:, :])
                        last.then_inc(pe["gatew"], 1)
                        te.wait_ge(dve["gatew"], 2)
                        free(path, st, 3)
                        for k in range(K):
                            last = nc.tensor.matmul(path.bank(st, 3)[:, 0:D], wmem_sb[:, k, :], gate_cT[:, k, :],
                                                    start=k == 0, stop=k == K - 1)
                        last.then_inc(pe["gatem"], 1)
                    elif kind == "tiles":
                        te.wait_ge(dve["mask"], 1)
                        free(path, st)
                        nc.tensor.matmul(path.bank(st)[0:1, 0:B * KT], tile_any[:, :], ident[0:B * KT, 0:B * KT],
                                         start=True, stop=True).then_inc(pe["mask"], 1)
                    elif kind == "y":
                        if c == 1:
                            te.wait_ge(dve["wmem"], 1)
                        te.wait_ge(dve["xT"], c)
                        free(path, st)
                        for k in range(K):
                            last = split_matmul(path.bank(st)[:, 0:N], lambda a: wmem_pair[:, a, k, :],
                                                lambda a: xT_pair[:, a, k, :], k == 0, k == K - 1)
                        last.then_inc(pe["y"], 1)
                    elif kind == "scores":
                        what, b, u = st[1:]
                        for t in range(T):
                            n = path.score_no(what, b, u, t)
                            if n >= 2:
                                te.wait_ge(act["exp"], n - 1)
                            toks = slice(t * P, (t + 1) * P)
                            if what == "ctx":
                                if t == 0:
                                    te.wait_ge(act["y"], path.at[("y", b)])
                                    te.wait_ge(dve["ctxT"], path.at[("ctxT", b)])
                                last = nc.tensor.matmul(SC[n % 2][:, :], yT[:, toks], ctxT[:, b, :],
                                                        start=True, stop=True)
                            else:
                                if path.nt == 1:
                                    kept = mask_bias[0:1, b * M + HOT * P:b * M + (HOT + 1) * P]
                                    bias = kept.rearrange("a (h k) -> a h k", h=1).to_broadcast([1, 4, P])
                                    nc.tensor.matmul(SC[n % 2][:, :].rearrange("p (h k) -> p h k", h=4),
                                                     ones_bf[0:1, :], bias, start=True, stop=False)
                                else:
                                    nc.tensor.matmul(SC[n % 2][:, :], ones_bf[0:1, :],
                                                     mask_bias[0:1, b * M:(b + 1) * M], start=True, stop=False)
                                if t == 0:
                                    te.wait_ge(dve["q"], path.at[("q", b, (u * path.heads) // 4)])
                                    if u == 0:
                                        keys = path.at[("k", path.keys_of(b), PAIRS - 1)]
                                        te.wait_ge(act["k"], keys)
                                        te.wait_ge(dve["k"], keys)
                                        te.wait_ge(const_ready, 6)
                                if path.nt == 1:
                                    for i in range(2):
                                        last = nc.tensor.matmul(
                                            SC[n % 2][:, i * 2 * P:(i + 1) * 2 * P], q_sb[:, 2 * u + i, toks],
                                            k_split[:, 2 * u + i, b, :, :], start=False, stop=i == 1)
                                else:
                                    last = nc.tensor.matmul(
                                        SC[n % 2][:, :].rearrange("p (s k) -> p s k", s=KT), q_sb[:, u // 2, toks],
                                        k_split[:, u // 2, :, u % 2, :], start=False, stop=True)
                            last.then_inc(pe["scores"], 1)
                    elif kind == "spread":
                        for t in range(T):
                            n = path.score_no(*st[1:], t)
                            te.wait_ge(pool["probs"], n + 1)
                            if n >= 2:
                                te.wait_ge((act, dve)[t]["spread"], n // 2)
                            for j in range(4):
                                last = nc.tensor.transpose(SPREAD[n % 2][:, j * P:(j + 1) * P],
                                                           probs[:, n % RING, j * P:(j + 1) * P], ident[:, :])
                            last.then_inc(pe["spread"], 1)
                    elif kind == "u":
                        b = st[1]
                        m = path.at[("spread", "ctx", b, 0)]
                        te.wait_ge(act["spread"], m)
                        te.wait_ge(dve["spread"], m)
                        free(path, st)
                        for j in range(KT):
                            last = nc.tensor.matmul(path.bank(st)[:, 0:N], ctx_sb[:, b * KT + j, :],
                                                    ctx_probsT[:, j, :], start=j == 0, stop=j == KT - 1)
                        last.then_inc(pe["u"], 1)
                    elif kind == "gate":
                        te.wait_ge(dve["u"], c)
                        if c == 1:
                            te.wait_ge(dve["gatew"], 4)
                            te.wait_ge(dve["bgate"], 1)
                        for t in range(T):
                            toks = slice(t * P, (t + 1) * P)
                            free(path, st, t)
                            out_b = path.bank(st, t)
                            split_matmul(out_b[:, :], lambda a: uT_pair[:, a, toks], lambda a: gate_mem_pair[:, a, :],
                                         True, False)
                            nc.tensor.matmul(out_b[:, 0:D], ones_r[:, :], bgate_parts[:, :], start=False, stop=False)
                            for k in range(K):
                                last = split_matmul(out_b[:, 0:D], lambda a: xT_pair[:, a, k, toks],
                                                    lambda a: gate_xT_pair[:, a, k, :], False, k == K - 1)
                            last.then_inc(pe["gate"], 1)
                    elif kind in ("xhT", "h2T"):
                        te.wait_ge(pool["affine"], c if kind == "xhT" else B + c)
                        free(path, st)
                        normed = xhat if kind == "xhT" else x2hat_buf(c - 1)
                        for k in range(K):
                            for t in range(T):
                                last = nc.tensor.transpose(path.bank(st)[:, k * N + t * P:k * N + (t + 1) * P],
                                                           normed[:, t, k:D:K], ident[:, :])
                        last.then_inc(pe[kind], 1)
                    elif kind == "k":
                        b, pair = st[1:]
                        if c == 1:
                            te.wait_ge(w_in["wkv"], 16)
                            te.wait_ge(dve["ctxT"], B)
                        free(path, st)
                        keys = ctxT[:, :, HOT * P:M] if b == "hot" else ctxT[:, b, :]
                        nc.tensor.matmul(
                            path.bank(st)[:, :].rearrange("p (s n) -> p s n", s=KT) if b == "hot"
                            else path.bank(st)[:, :],
                            wkv_sb[:, pair * P:(pair + 1) * P], keys, start=True, stop=True).then_inc(pe["k"], 1)
                    elif kind == "v":
                        b, s, h = st[1:]
                        free(path, st)
                        keys = ctxT[:, s, HOT * P:M] if b == "hot" else ctxT[:, b, s * P:(s + 1) * P]
                        nc.tensor.matmul(path.bank(st)[:, :], keys,
                                         wkv_sb[:, INNER + h * BANK:INNER + (h + 1) * BANK],
                                         start=True, stop=True).then_inc(pe["v"], 1)
                    elif kind == "q":
                        b, j = st[1:]
                        if j == 0:
                            te.wait_ge(dve["xhT"], path.at[("xhT", b)])
                            if b == 0:
                                te.wait_ge(dve["wsplit"], 2)
                        free(path, st)
                        for i in range(2):
                            pair = slice((2 * j + i) * P, (2 * j + i + 1) * P)
                            for k in range(K):
                                last = split_matmul(path.bank(st)[:, i * N:(i + 1) * N],
                                                    lambda a: wq_p[:, a, k, pair], lambda a: xhT_pair[:, a, k, :],
                                                    k == 0, k == K - 1)
                        last.then_inc(pe["q"], 1)
                    elif kind == "av":
                        b, u = st[1:]
                        m = path.at[("spread", "head", b, u)]
                        unit = b * path.units + u
                        te.wait_ge(act["spread"], m)
                        te.wait_ge(dve["spread"], m)
                        if u == 0:
                            values = path.at[("v", path.keys_of(b), b if path.nt == 1 else KT - 1, 1)] // 2
                            te.wait_ge(act["v"], values)
                            te.wait_ge(dve["v"], values)
                        if b == 0 and u == 0:
                            for s, v in path.was_read(*path.last_use[CONTEXT.name]):
                                te.wait_ge(s, v)
                        if u % path.nt == 0:
                            done = path.quads(b, u) - (1 if path.nt == 1 else 0)
                            if done:
                                te.wait_ge(dve["o"], done)
                        if path.nt == 1:
                            for h in range(4):
                                head, half = 4 * u + h, h % 2
                                last = nc.tensor.matmul(
                                    CONTEXT[half * DH:(half + 1) * DH, (h // 2) * N:(h // 2 + 1) * N],
                                    v_sb[:, b, head * DH:(head + 1) * DH], probsT[:, unit % 2, h, :],
                                    start=True, stop=True)
                        else:
                            half, col = u % 2, (u % 4) // 2
                            for s in range(KT):
                                last = nc.tensor.matmul(
                                    CONTEXT[half * DH:(half + 1) * DH, col * N:(col + 1) * N],
                                    v_sb[:, s, u * DH:(u + 1) * DH], probsT[:, unit % 2, s, :],
                                    start=s == 0, stop=s == KT - 1)
                        last.then_inc(pe["av"], 1)
                    elif kind == "wo":
                        b, g = st[1:]
                        te.wait_ge(dve["o"], c)
                        if b == 0 and g == 0:
                            te.wait_ge(pool["wsplit"], 2)
                            for s, v in path.was_read(*path.last_use[PROJ.name]):
                                te.wait_ge(s, v)
                        if b and g == 0:
                            te.wait_ge(dve["wo"], b)
                        for t in range(T):
                            toks = slice(t * P, (t + 1) * P)
                            for i in range(2):
                                last = split_matmul(PROJ[:, t * D:(t + 1) * D],
                                                    lambda a: oT_pair[:, a, (c - 1) % 2, i, toks],
                                                    lambda a: wo_p[:, a, 2 * g + i, :],
                                                    g == 0 and t == 0 and i == 0, g == 3 and t == T - 1 and i == 1)
                        last.then_inc(pe["wo"], 1)
                    elif kind == "ff1":
                        f, m = st[1:]
                        if m == 0:
                            te.wait_ge(dve["h2T"], 2 * (f + 1))
                            if f == 0:
                                te.wait_ge(dve["wsplit"], 4)
                        free(path, st)
                        for k in range(K):
                            last = split_matmul(path.bank(st)[:, :], lambda a: w1_p[a][:, k, m * P:(m + 1) * P],
                                                lambda a: h2T_pair[:, a, k, :], k == 0, k == K - 1)
                        last.then_inc(pe["ff1"], 1)
                    elif kind == "ff2":
                        f, i = st[1:]
                        toks = slice(i * P, (i + 1) * P)
                        if i == 0 and f == 0:
                            te.wait_ge(dve["wsplit"], 6)
                        free(path, st)
                        for m in range(FM):
                            if i == 0:
                                te.wait_ge(dve["gelu"], FM * f + m + 1)
                            last = split_matmul(path.bank(st)[:, 0:D], lambda a: gelu_pair[:, m, a, toks],
                                                lambda a: w2_p[:, a, m, :], m == 0, m == FM - 1)
                        last.then_inc(pe["ff2"], 1)

            te.wait_ge(warm_ready, 1)
            for _ in range(WARM_UP):
                nc.tensor.matmul(CONTEXT[:, :], warm[:, 0:P], warm[:, :], start=True, stop=True)
            te.wait_ge(const_ready, 3)
            run(paths[1], PRO)
            te.wait_ge(flag_ready, 1)
            te.wait_ge(act["mask"], 1)
            short = te.value_load(short_flag[0:1, 0:1], min_val=0, max_val=1)
            with te.If(short == 1):
                run(paths[1], paths[1].plan[len(PRO):])
            with te.Else():
                run(paths[KT], paths[KT].plan[len(PRO):])


_INS = ['x', 'ctx_1024', 'mask_BxS2_bk0', 'L0_xattn_W_mem', 'L0_xattn_W_gate', 'L0_xattn_b_gate', 'L0_xattn_norm_w',
        'L1_xattn_ln_q_g', 'L1_xattn_ln_q_b', 'L1_xattn_Wq', 'L1_xattn_Wkv', 'L1_xattn_Wo', 'L1_xattn_attn_gate',
        'L1_xattn_ln_ff_g', 'L1_xattn_ln_ff_b', 'L1_xattn_W1', 'L1_xattn_W2', 'L1_xattn_ff_gate']


def kernel(**inputs):
    import numpy as _np
    import concourse.bacc as _bacc
    from concourse import mybir as _mybir
    from concourse.bass_utils import run_bass_kernel_spmd as _run

    nc = _bacc.Bacc("TRN2", target_bir_lowering=False, num_devices=1)
    arrays, args = {}, []
    for name in _INS:
        a = _np.ascontiguousarray(inputs[name])
        arrays[f"in_{name}_dram"] = a
        args.append(nc.dram_tensor(f"in_{name}_dram", a.shape, _mybir.dt.from_np(a.dtype), kind="ExternalInput").ap())
    shape = inputs['x'].shape
    args.append(nc.dram_tensor("out_0_dram", shape, _mybir.dt.float32, kind="ExternalOutput").ap())
    gated_attention_block(nc, *args)
    r = _run(nc, [arrays], core_ids=[0])
    return r.results[0]["out_0_dram"]
```
